# Optimizing a Trainium2 kernel written in Bass

```python
import numpy as np
import jax
import jax.numpy as jnp

def _softmax(x, axis=-1):
    return jax.nn.softmax(x, axis=axis)

def _gelu(x):
    return jax.nn.gelu(x, approximate=True)

def _silu(x):
    return jax.nn.silu(x)

def _sigmoid(x):
    return jax.nn.sigmoid(x)

def _layernorm(x, axis=-1, eps=1e-05):
    m = jnp.mean(x, axis=axis, keepdims=True)
    v = jnp.var(x, axis=axis, keepdims=True)
    return (x - m) / jnp.sqrt(v + eps)

def _scatter_add(tgt, idx, src, axis=0):
    return tgt.at[idx].add(src)

def _segment_sum(src, seg, n):
    return jax.ops.segment_sum(src, seg, n)
kernel_name = 'mk_conv_seq_d2_conv_nchw512_r2_c64233'

def setup_inputs(seed: int=0):
    np.random.seed(seed)
    _w = jnp.asarray

    def _rec_inputs():
        import jax
        import jax.numpy as jnp
        _gk = jax.random.key(seed)
        x = -9.26e-05 + 0.9999 * jax.random.normal(jax.random.fold_in(_gk, 1), (8, 256, 48, 48), jnp.float32)
        return x
    x = _rec_inputs()

    def _L0_conv_setup():
        import jax, jax.numpy as jnp
        import numpy as np
        HEADS = 8

        def _conv1x1(x, W, b):
            return jnp.einsum('nchw,oc->nohw', x, W) + b[None, :, None, None]
        key = jax.random.key(seed)
        ks = jax.random.split(key, 5)
        n, c, h, w = (8, 256, 48, 48)
        kc, vc = (256, 256)
        s = 0.02
        return {'x': jax.random.normal(ks[0], (n, c, h, w), jnp.float32), 'Wk': jax.random.normal(ks[1], (kc, c), jnp.float32) * s, 'bk': jnp.zeros((kc,), jnp.float32), 'Wq': jax.random.normal(ks[2], (kc, c), jnp.float32) * s, 'bq': jnp.zeros((kc,), jnp.float32), 'Wv': jax.random.normal(ks[3], (vc, c), jnp.float32) * s, 'bv': jnp.zeros((vc,), jnp.float32), 'Wp': jax.random.normal(ks[4], (c, vc), jnp.float32) * s, 'bp': jnp.zeros((c,), jnp.float32)}
    _L0_conv_all = _L0_conv_setup()
    _L0_conv_in = {k: v for k, v in _L0_conv_all.items() if k in ('Wk', 'bk', 'Wq', 'bq', 'Wv', 'bv', 'Wp', 'bp')}
    del _L0_conv_all

    def _L1_conv_setup():
        import jax, jax.numpy as jnp
        import numpy as np
        DIM = 8
        HEADS = 32
        INNER = HEADS * DIM
        CIN = 256
        COUT = 256
        SCALE = 5
        G = 3 * HEADS
        EPS_ATT = 1e-15
        EPS_BN = 1e-05

        def _aggreg(qkv, w_dw, w_pw):
            y = jax.lax.conv_general_dilated(qkv, w_dw, window_strides=(1, 1), padding=[(2, 2), (2, 2)], dimension_numbers=('NCHW', 'OIHW', 'NCHW'), feature_group_count=3 * INNER)
            B, C, H, W = y.shape
            yg = y.reshape(B, G, DIM, H, W)
            out = jnp.einsum('gok,bgkhw->bgohw', w_pw, yg)
            return out.reshape(B, C, H, W)

        def _relu_linear_att(qkv):
            B, C, H, W = qkv.shape
            N = H * W
            qkv = qkv.astype(jnp.float32).reshape(B, -1, 3 * DIM, N)
            q = jax.nn.relu(qkv[:, :, :DIM])
            k = jax.nn.relu(qkv[:, :, DIM:2 * DIM])
            v = qkv[:, :, 2 * DIM:]
            v1 = jnp.concatenate([v, jnp.ones_like(v[:, :, :1])], axis=2)
            vk = jnp.einsum('bhdn,bhen->bhde', v1, k)
            out = jnp.einsum('bhde,bhen->bhdn', vk, q)
            out = out[:, :, :-1] / (out[:, :, -1:] + EPS_ATT)
            return out.reshape(B, -1, H, W)
        key = jax.random.key(seed)
        ks = jax.random.split(key, 7)
        B, H, W = (2, 64, 64)
        x = jax.random.normal(ks[0], (B, CIN, H, W), dtype=jnp.float32)
        w_qkv = jax.random.normal(ks[1], (3 * INNER, CIN), dtype=jnp.float32) * 0.02
        w_dw = jax.random.normal(ks[2], (3 * INNER, 1, SCALE, SCALE), dtype=jnp.float32) * 0.05
        w_pw = jax.random.normal(ks[3], (G, DIM, DIM), dtype=jnp.float32) * 0.1
        w_proj = jax.random.normal(ks[4], (COUT, 2 * INNER), dtype=jnp.float32) * 0.02
        bn_gamma = jnp.ones((COUT,), dtype=jnp.float32)
        bn_beta = jnp.zeros((COUT,), dtype=jnp.float32)
        return {'x': x, 'w_qkv': w_qkv, 'w_dw': w_dw, 'w_pw': w_pw, 'w_proj': w_proj, 'bn_gamma': bn_gamma, 'bn_beta': bn_beta}
    _L1_conv_all = _L1_conv_setup()
    _L1_conv_in = {k: v for k, v in _L1_conv_all.items() if k in ('w_qkv', 'w_dw', 'w_pw', 'w_proj', 'bn_gamma', 'bn_beta')}
    del _L1_conv_all
    return {'x': x, 'L0_conv_Wk': _L0_conv_in['Wk'], 'L0_conv_bk': _L0_conv_in['bk'], 'L0_conv_Wq': _L0_conv_in['Wq'], 'L0_conv_bq': _L0_conv_in['bq'], 'L0_conv_Wv': _L0_conv_in['Wv'], 'L0_conv_bv': _L0_conv_in['bv'], 'L0_conv_Wp': _L0_conv_in['Wp'], 'L0_conv_bp': _L0_conv_in['bp'], 'L1_conv_w_qkv': _L1_conv_in['w_qkv'], 'L1_conv_w_dw': _L1_conv_in['w_dw'], 'L1_conv_w_pw': _L1_conv_in['w_pw'], 'L1_conv_w_proj': _L1_conv_in['w_proj'], 'L1_conv_bn_gamma': _L1_conv_in['bn_gamma'], 'L1_conv_bn_beta': _L1_conv_in['bn_beta']}

def reference(x, L0_conv_Wk, L0_conv_bk, L0_conv_Wq, L0_conv_bq, L0_conv_Wv, L0_conv_bv, L0_conv_Wp, L0_conv_bp, L1_conv_w_qkv, L1_conv_w_dw, L1_conv_w_pw, L1_conv_w_proj, L1_conv_bn_gamma, L1_conv_bn_beta):
    import jax
    import jax.numpy as jnp

    def _L0_conv_ref(x, Wk, bk, Wq, bq, Wv, bv, Wp, bp):
        import jax, jax.numpy as jnp
        import numpy as np
        HEADS = 8

        def _conv1x1(x, W, b):
            return jnp.einsum('nchw,oc->nohw', x, W) + b[None, :, None, None]
        n, c, h, w = x.shape
        kc, vc = (Wk.shape[0], Wv.shape[0])
        hk, hv = (kc // HEADS, vc // HEADS)
        hw = h * w
        keys = _conv1x1(x, Wk, bk).reshape(n, HEADS, hk, hw)
        queries = _conv1x1(x, Wq, bq).reshape(n, HEADS, hk, hw)
        values = _conv1x1(x, Wv, bv).reshape(n, HEADS, hv, hw)
        keyS = jax.nn.softmax(keys, axis=3)
        queryS = jax.nn.softmax(queries, axis=2)
        context = jnp.einsum('nhkp,nhvp->nhkv', keyS, values)
        attended = jnp.einsum('nhkv,nhkp->nhvp', context, queryS)
        aggregated = attended.reshape(n, vc, h, w)
        out = _conv1x1(aggregated, Wp, bp) + x
        return out

    def _L1_conv_ref(x, w_qkv, w_dw, w_pw, w_proj, bn_gamma, bn_beta):
        import jax, jax.numpy as jnp
        import numpy as np
        DIM = 8
        HEADS = 32
        INNER = HEADS * DIM
        CIN = 256
        COUT = 256
        SCALE = 5
        G = 3 * HEADS
        EPS_ATT = 1e-15
        EPS_BN = 1e-05

        def _aggreg(qkv, w_dw, w_pw):
            y = jax.lax.conv_general_dilated(qkv, w_dw, window_strides=(1, 1), padding=[(2, 2), (2, 2)], dimension_numbers=('NCHW', 'OIHW', 'NCHW'), feature_group_count=3 * INNER)
            B, C, H, W = y.shape
            yg = y.reshape(B, G, DIM, H, W)
            out = jnp.einsum('gok,bgkhw->bgohw', w_pw, yg)
            return out.reshape(B, C, H, W)

        def _relu_linear_att(qkv):
            B, C, H, W = qkv.shape
            N = H * W
            qkv = qkv.astype(jnp.float32).reshape(B, -1, 3 * DIM, N)
            q = jax.nn.relu(qkv[:, :, :DIM])
            k = jax.nn.relu(qkv[:, :, DIM:2 * DIM])
            v = qkv[:, :, 2 * DIM:]
            v1 = jnp.concatenate([v, jnp.ones_like(v[:, :, :1])], axis=2)
            vk = jnp.einsum('bhdn,bhen->bhde', v1, k)
            out = jnp.einsum('bhde,bhen->bhdn', vk, q)
            out = out[:, :, :-1] / (out[:, :, -1:] + EPS_ATT)
            return out.reshape(B, -1, H, W)
        residual = x
        qkv = jnp.einsum('oc,bchw->bohw', w_qkv, x)
        qkv_ms = jnp.concatenate([qkv, _aggreg(qkv, w_dw, w_pw)], axis=1)
        out = _relu_linear_att(qkv_ms).astype(qkv_ms.dtype)
        out = jnp.einsum('oc,bchw->bohw', w_proj, out)
        mean = jnp.mean(out, axis=(0, 2, 3), keepdims=True)
        var = jnp.var(out, axis=(0, 2, 3), keepdims=True)
        out = (out - mean) * jax.lax.rsqrt(var + EPS_BN)
        out = out * bn_gamma[None, :, None, None] + bn_beta[None, :, None, None]
        return out + residual

    def _gn(v, G=32, eps=1e-05):
        B_, C_, H_, W_ = v.shape
        g = v.reshape(B_, G, C_ // G, H_, W_)
        m = jnp.mean(g, axis=(2, 3, 4), keepdims=True)
        s = jnp.var(g, axis=(2, 3, 4), keepdims=True)
        return ((g - m) / jnp.sqrt(s + eps)).reshape(v.shape)

    def _ln_c(v, eps=1e-06):
        m = jnp.mean(v, axis=1, keepdims=True)
        s = jnp.var(v, axis=1, keepdims=True)
        return (v - m) / jnp.sqrt(s + eps)

    def _ln_t(v, eps=1e-05):
        m = jnp.mean(v, axis=-1, keepdims=True)
        s = jnp.var(v, axis=-1, keepdims=True)
        return (v - m) / jnp.sqrt(s + eps)

    def _to_tokens(v):
        B_, C_, H_, W_ = v.shape
        return v.reshape(B_, C_, H_ * W_).transpose(0, 2, 1)

    def _from_tokens(t, like):
        B_, C_, H_, W_ = like.shape
        return t.transpose(0, 2, 1).reshape(B_, C_, H_, W_)
    x = _L0_conv_ref(x, L0_conv_Wk, L0_conv_bk, L0_conv_Wq, L0_conv_bq, L0_conv_Wv, L0_conv_bv, L0_conv_Wp, L0_conv_bp)
    x = _L1_conv_ref(x, L1_conv_w_qkv, L1_conv_w_dw, L1_conv_w_pw, L1_conv_w_proj, L1_conv_bn_gamma, L1_conv_bn_beta)
    return x

_drawn_inputs = setup_inputs


def setup_inputs(seed=0):
    import zlib

    import numpy as np

    out = dict(_drawn_inputs(seed))
    spreads = {'L0_conv_bk': (0.0, 0.8),
     'L0_conv_bq': (0.0, 0.8),
     'L0_conv_bv': (0.0, 0.1),
     'L0_conv_bp': (0.0, 0.1),
     'L1_conv_bn_gamma': (1.0, 0.2),
     'L1_conv_bn_beta': (0.0, 0.1)}
    factors = {'L0_conv_Wk': 8.0, 'L0_conv_Wq': 8.0}
    for name, (base, spread) in spreads.items():
        noise = np.random.default_rng([zlib.crc32(name.encode()), seed]).standard_normal(out[name].shape)
        drawn = base * np.exp(spread * noise) if base else spread * noise
        out[name] = jnp.asarray(drawn.astype(out[name].dtype))
    for name, factor in factors.items():
        out[name] = (out[name] * factor).astype(out[name].dtype)
    return out
```

```python
from contextlib import ExitStack

import concourse.bass as bass
from concourse import mybir
from concourse.alu_op_type import AluOpType as ALU

ACT = mybir.ActivationFunctionType
F32 = mybir.dt.float32
AX = mybir.AxisListType

P = 128
NIMG, C, H, W = 8, 256, 48, 48
HW = H * W
CT = C // P
CHUNK = 8 * W
NCH = HW // CHUNK

HEADS0, HD0 = 8, 32
PAIR = 2 * P
NPAIR = HW // PAIR

DIM, SCALE5, PAD = 8, 5, 2
HP, WP = H + 2 * PAD, W + 2 * PAD
NU = 6
PARTS = (1, 2, 1, 2, 0, 0)
HALVES = (0, 0, 1, 1, 0, 1)
EPS_ATT, EPS_BN = 1e-15, 1e-5
DY_PE = 3
NSH = 4
HALF = H // 2
RROWS = HALF + DY_PE - 1
DVE_TAPS = [(dy, dx) for dy in range(SCALE5) for dx in range(SCALE5) if not (dy < DY_PE and dx < NSH)]
NT = len(DVE_TAPS)
DG, AG = 10, HW // (2 * P)
DFIRST = PAD * WP - (DG * 2 * P - H * WP) // 2
assert DFIRST >= 0 and DFIRST + DG * 2 * P <= HP * WP and DFIRST + DG * 2 * P >= (PAD + H) * WP
PRODUCTS = ((0, 0, 0), (0, 1, 0), (2, 0, 1), (2, 1, 1))
SEG = (0, DG, DG + AG, 2 * DG + AG)
NTR = 2 * (DG + AG)


def slot_of(product):
    _, source, half = PRODUCTS[product]
    return 2 * source + half


def wait_count(eng, sem, value):
    if isinstance(value, int) and value <= 0:
        return
    eng.wait_ge(sem, value)


def settle(eng, value):
    return value if isinstance(value, int) else eng.snap(value)


def image_of(array, i):
    return array[i] if isinstance(i, int) else array[bass.ds(i, 1)].rearrange("o p c t -> p (o c) t")


def phase_l0(nc, dram, sem):
    with ExitStack() as ctx:
        def sb(name, shape):
            return ctx.enter_context(nc.sbuf_tensor(name, shape, F32))

        def ps(name, shape):
            return ctx.enter_context(nc.psum_tensor(name, shape, F32))

        xs = sb("xs", [P, 2, CT, HW])
        wk = sb("wk", [P, CT, C])
        wqv = sb("wqv", [P, CT, 2 * C])
        wp = sb("wp", [P, CT, C])
        bqv = sb("bqv", [P, 2, C])
        bkp = sb("bkp", [P, 2, CT])
        ident = sb("ident0", [P, P])
        mask32 = sb("mask32", [P, P])
        keys = sb("keys", [P, CT, HW])
        nmax = sb("nmax", [P, CT])
        ksum = sb("ksum", [P, CT])
        rk = sb("rk", [P, CT])
        vT = sb("vT", [P, HW // P, C])
        ekT = sb("ekT", [P, 2, 2, C])
        ctxm = sb("ctxm", [P, CT, P])
        mt = sb("mt", [P, CT, C])
        qs = sb("qs", [P, 3, 2, HEADS0, HD0])
        qmx = sb("qmx", [P, 2, 2 * HEADS0])
        qsm = sb("qsm", [P, 2, 2 * HEADS0])
        qrc = sb("qrc", [P, 2, 2 * HEADS0])
        qn = sb("qn", [P, 2, CT, PAIR])

        kp = ps("kp", [P, 2, 512])
        vp = ps("vp", [P, 2, 512])
        ep = ps("ep", [P, 2, 512])
        xp = ps("xp", [P, 2, 512])

        def vbank(n):
            return vp[:, n % 2, :].rearrange("p (t c) -> p t c", t=2)

        def ebank(n):
            return ep[:, n % 2, :].rearrange("p (t c) -> p t c", t=2)

        (w_in, x_in0, x_in1, x_out0, x_out1, k_filled, k_freed, nmax_ready, exp_done, v_filled, v_freed,
         e_filled, e_freed, ctx_step, ctx_masked, rk_ready, m_filled, mt_ready, q_maxed,
         q_shifted, q_exp, q_summed, q_recip, q_ready, x_filled, x1_done) = (
            sem(f"l0_{n}") for n in (
                "w_in x_in0 x_in1 x_out0 x_out1 k_filled k_freed nmax_ready exp_done v_filled v_freed "
                "e_filled e_freed ctx_step ctx_masked rk_ready m_filled mt_ready q_maxed "
                "q_shifted q_exp q_summed q_recip q_ready x_filled x1_done").split())
        x_in, x_out = (x_in0, x_in1), (x_out0, x_out1)
        NW = 7
        QN = NPAIR

        block = ctx.enter_context(nc.Block())

        @block.sync
        def _(sp):
            for par in range(2):
                sp.dma_start(xs[:, par], dram["x"][par]).then_inc(x_in[par], 16)
                if par == 0:
                    for dst, name in ((wk, "wk"), (wqv, "wqv"), (wp, "wp"), (bqv, "bqv"), (bkp, "bkp"),
                                      (ident, "ident"), (mask32, "mask32")):
                        sp.dma_start(dst[:], dram[name]).then_inc(w_in, 16)
            with sp.Fori(0, NIMG // 2 - 1) as it:
                for par in range(2):
                    written = sp.snap((2 * it + par + 1) * NPAIR)
                    stored = sp.snap((it + 1) * 16)
                    here = sp.snap(2 * it + par)
                    there = sp.snap(2 * it + par + 2)
                    sp.wait_ge(x1_done, written)
                    sp.dma_start(image_of(dram["x1"], here),
                                 xs[:, par]).then_inc(x_out[par], 16)
                    sp.wait_ge(x_out[par], stored)
                    sp.dma_start(xs[:, par], image_of(dram["x"], there)).then_inc(x_in[par], 16)
            for par in range(2):
                n = NIMG - 2 + par
                sp.wait_ge(x1_done, (n + 1) * NPAIR)
                sp.dma_start(dram["x1"][n], xs[:, par]).then_inc(x_out[par], 16)
            for par in range(2):
                sp.wait_ge(x_out[par], 16 * NIMG // 2)

        @block.tensor
        def _(pe):
            pe.wait_ge(w_in, 16 * NW)

            def images(it):
                for par in range(2):
                    n = 2 * it + par
                    x = xs[:, par]
                    pe.wait_ge(x_in[par], (it + 1) * 16)
                    for g in range(CT * NCH):
                        m, c = g // NCH, g % NCH
                        wait_count(pe, k_freed, n * (CT * NCH) + (g - 1 if g >= 2 else 0))
                        for kc in range(CT):
                            mm = nc.tensor.matmul(kp[:, g % 2, :CHUNK], wk[:, kc, m * P:(m + 1) * P],
                                                  x[:, kc, c * CHUNK:(c + 1) * CHUNK],
                                                  start=(kc == 0), stop=(kc == CT - 1))
                        mm.then_inc(k_filled, 1)

                    def token_major(g, first, cols):
                        k = first + g
                        wait_count(pe, v_freed, n * (2 * NPAIR) + (k - 1 if k >= 2 else 0))
                        for t in range(2):
                            for kc in range(CT):
                                mm = nc.tensor.matmul(vbank(k)[:, t, :],
                                                      x[:, kc, (2 * g + t) * P:(2 * g + t + 1) * P],
                                                      wqv[:, kc, cols:cols + C], start=(kc == 0), stop=(kc == CT - 1))
                        mm.then_inc(v_filled, 1)

                    for g in range(NPAIR):
                        token_major(g, 0, C)

                    def context(g):
                        pe.wait_ge(e_freed, n * (2 * NPAIR) + g + 1)
                        if g == 0:
                            pe.wait_ge(v_freed, n * (2 * NPAIR) + NPAIR)
                            wait_count(pe, x1_done, n * NPAIR)
                        for t in range(2):
                            for h in range(CT):
                                mm = nc.tensor.matmul(xp[:, 0, h * P:(h + 1) * P],
                                                      vT[:, 2 * g + t, h * P:(h + 1) * P],
                                                      ekT[:, g % 2, t, h * P:(h + 1) * P],
                                                      start=(g == 0 and t == 0 and h == 0),
                                                      stop=(g == NPAIR - 1 and t == 1), skip_group_check=True)
                        mm.then_inc(ctx_step, 1)

                    pe.wait_ge(exp_done, n * CT + CT)
                    for g in range(NPAIR):
                        wait_count(pe, e_freed, n * (2 * NPAIR) + (g - 1 if g >= 2 else 0))
                        for t in range(2):
                            for h in range(CT):
                                mm = nc.tensor.transpose(ebank(g)[:, t, h * P:(h + 1) * P],
                                                         keys[:, h, (2 * g + t) * P:(2 * g + t + 1) * P], ident[:])
                        mm.then_inc(e_filled, 1)
                        if g >= 1:
                            context(g - 1)
                    context(NPAIR - 1)
                    for g in range(2):
                        token_major(g, QN, 0)
                    pe.wait_ge(ctx_masked, n + 1)
                    for h in range(CT):
                        mm = nc.tensor.matmul(xp[:, 1, h * C:(h + 1) * C], ctxm[:, h], wp[:, h],
                                              start=True, stop=True, skip_group_check=True)
                    mm.then_inc(m_filled, 1)

                    def x1_group(g):
                        pe.wait_ge(e_freed, n * (2 * NPAIR) + QN + g + 1)
                        if g == 0:
                            pe.wait_ge(mt_ready, n + 1)
                        if g >= 2:
                            pe.wait_ge(x1_done, n * NPAIR + g - 1)
                        for m in range(CT):
                            for kc in range(CT):
                                mm = nc.tensor.matmul(xp[:, g % 2, m * PAIR:(m + 1) * PAIR],
                                                      mt[:, kc, m * P:(m + 1) * P], qn[:, g % 2, kc, :],
                                                      start=(kc == 0), stop=(kc == CT - 1), skip_group_check=True)
                        mm.then_inc(x_filled, 1)

                    for g in range(NPAIR):
                        if g + 2 < NPAIR:
                            token_major(g + 2, QN, 0)
                        k = QN + g
                        pe.wait_ge(q_ready, n * NPAIR + g + 1)
                        pe.wait_ge(e_freed, n * (2 * NPAIR) + k - 1)
                        for t in range(2):
                            for h in range(CT):
                                src = qs[:, g % 3, t, 4 * h:4 * h + 4, :].rearrange("p a b -> p (a b)")
                                mm = nc.tensor.transpose(ebank(k)[:, h, t * P:(t + 1) * P], src, ident[:])
                        mm.then_inc(e_filled, 1)
                        if g >= 1:
                            x1_group(g - 1)
                    x1_group(NPAIR - 1)

            images(0)
            with pe.Fori(1, NIMG // 2) as it:
                images(it)

        @block.scalar
        def _(act):
            act.wait_ge(w_in, 16 * NW)

            def images(it):
                for par in range(2):
                    n = 2 * it + par
                    wait_count(act, ctx_masked, n)
                    for g in range(CT * NCH):
                        m, c = g // NCH, g % NCH
                        act.wait_ge(k_filled, n * (CT * NCH) + g + 1)
                        nc.scalar.activation(keys[:, m, c * CHUNK:(c + 1) * CHUNK], kp[:, g % 2, :CHUNK],
                                             ACT.Identity, bias=bkp[:, 0, m:m + 1]).then_inc(k_freed, 1)
                    wait_count(act, rk_ready, n)
                    for m in range(CT):
                        act.wait_ge(nmax_ready, n * CT + m + 1)
                        nc.scalar.activation(keys[:, m, :], keys[:, m, :], ACT.Exp, bias=nmax[:, m:m + 1],
                                             accum_out=ksum[:, m:m + 1]).then_inc(exp_done, 1)
                    for g in range(NPAIR):
                        act.wait_ge(e_filled, n * (2 * NPAIR) + g + 1)
                        wait_count(act, ctx_step, n * NPAIR + (g - 1 if g >= 2 else 0))
                        nc.scalar.copy(ekT[:, g % 2], ebank(g)).then_inc(e_freed, 1)
                    act.wait_ge(m_filled, n + 1)
                    act.wait_ge(rk_ready, n + 1)
                    wait_count(act, x_filled, n * NPAIR)
                    for h in range(CT):
                        last = nc.scalar.activation(mt[:, h], xp[:, 1, h * C:(h + 1) * C], ACT.Copy, scale=rk[:, h:h + 1])
                    last.then_inc(mt_ready, 1)

                    def exp_q(g):
                        act.wait_ge(q_shifted, n * NPAIR + g + 1)
                        nc.scalar.activation(qs[:, g % 3], qs[:, g % 3], ACT.Exp).then_inc(q_exp, 1)

                    exp_q(0)
                    for g in range(NPAIR):
                        if g + 1 < NPAIR:
                            exp_q(g + 1)
                        k = QN + g
                        act.wait_ge(e_filled, n * (2 * NPAIR) + k + 1)
                        wait_count(act, x_filled, n * NPAIR + (g - 1 if g >= 2 else 0))
                        nc.scalar.copy(qn[:, g % 2], ebank(k)).then_inc(e_freed, 1)

            images(0)
            with act.Fori(1, NIMG // 2) as it:
                images(it)

        @block.vector
        def _(dve):
            dve.wait_ge(w_in, 16 * NW)

            def images(it):
                for par in range(2):
                    n = 2 * it + par
                    wait_count(dve, exp_done, n * CT)
                    for m in range(CT):
                        dve.wait_ge(k_freed, n * (CT * NCH) + (m + 1) * NCH)
                        nc.vector.tensor_reduce(nmax[:, m:m + 1], keys[:, m, :], AX.X, ALU.max,
                                                negate=True).then_inc(nmax_ready, 1)
                    bias = {"q": bqv[:, 0:1, :].to_broadcast([P, 2, C]), "v": bqv[:, 1:2, :].to_broadcast([P, 2, C])}
                    for g in range(NPAIR):
                        dve.wait_ge(v_filled, n * (2 * NPAIR) + g + 1)
                        nc.vector.tensor_tensor(vT[:, 2 * g:2 * g + 2, :], vbank(g), bias["v"], ALU.add).then_inc(v_freed, 1)
                    dve.wait_ge(exp_done, n * CT + CT)
                    wait_count(dve, mt_ready, n)
                    nc.vector.reciprocal(rk[:], ksum[:]).then_inc(rk_ready, 1)
                    dve.wait_ge(ctx_step, (n + 1) * NPAIR)
                    nc.vector.tensor_tensor(ctxm[:], xp[:, 0, 0:CT * P].rearrange("p (h k) -> p h k", h=CT),
                                            mask32[:].rearrange("p (o k) -> p o k", o=1).to_broadcast([P, CT, P]),
                                            ALU.mult).then_inc(ctx_masked, 1)

                    def shift_q(g):
                        k, r = QN + g, n * NPAIR
                        dve.wait_ge(v_filled, n * (2 * NPAIR) + k + 1)
                        if g >= 3:
                            dve.wait_ge(e_filled, n * (2 * NPAIR) + QN + g - 2)
                        q = qs[:, g % 3].rearrange("p t h d -> p t (h d)")
                        qh = qs[:, g % 3].rearrange("p t h d -> p (t h) d")
                        nc.vector.tensor_tensor(q, vbank(k), bias["q"], ALU.add).then_inc(v_freed, 1)
                        dve.wait_ge(v_freed, n * (2 * NPAIR) + k + 1)
                        nc.vector.tensor_reduce(qmx[:, g % 2], qh, AX.X, ALU.max).then_inc(q_maxed, 1)
                        dve.wait_ge(q_maxed, r + g + 1)
                        nc.vector.tensor_tensor(qh, qh, qmx[:, g % 2].rearrange("p (h o) -> p h o", o=1).to_broadcast(
                            [P, 2 * HEADS0, HD0]), ALU.subtract).then_inc(q_shifted, 1)

                    def normalise_q(g):
                        r = n * NPAIR
                        qh = qs[:, g % 3].rearrange("p t h d -> p (t h) d")
                        dve.wait_ge(q_exp, r + g + 1)
                        nc.vector.tensor_reduce(qsm[:, g % 2], qh, AX.X, ALU.add).then_inc(q_summed, 1)
                        dve.wait_ge(q_summed, r + g + 1)
                        nc.vector.reciprocal(qrc[:, g % 2], qsm[:, g % 2]).then_inc(q_recip, 1)
                        dve.wait_ge(q_recip, r + g + 1)
                        nc.vector.tensor_tensor(qh, qh, qrc[:, g % 2].rearrange("p (h o) -> p h o", o=1).to_broadcast(
                            [P, 2 * HEADS0, HD0]), ALU.mult).then_inc(q_ready, 1)

                    def add_x(g):
                        dve.wait_ge(x_filled, n * NPAIR + g + 1)
                        for m in range(CT):
                            xt = xs[:, par, m, g * PAIR:(g + 1) * PAIR]
                            last = nc.vector.scalar_tensor_tensor(out=xt, in0=xp[:, g % 2, m * PAIR:(m + 1) * PAIR],
                                                                  scalar=bkp[:, 1, m:m + 1], in1=xt,
                                                                  op0=ALU.add, op1=ALU.add)
                        last.then_inc(x1_done, 1)

                    shift_q(0)
                    shift_q(1)
                    for g in range(NPAIR):
                        normalise_q(g)
                        if g + 2 < NPAIR:
                            shift_q(g + 2)
                        if g >= 1:
                            add_x(g - 1)
                    add_x(NPAIR - 1)

            images(0)
            with dve.Fori(1, NIMG // 2) as it:
                images(it)


def phase_l1(nc, dram, sem, bnst):
    with ExitStack() as ctx:
        def sb(name, shape):
            return ctx.enter_context(nc.sbuf_tensor(name, shape, F32))

        def ps(name, shape):
            return ctx.enter_context(nc.psum_tensor(name, shape, F32))

        x1 = sb("x1", [P, CT, HW])
        wqkv = sb("wqkv", [P, CT, NU, P])
        wproj = sb("wproj", [P, 4, C])
        pwbd = sb("pwbd", [P, NU, P])
        dws = sb("dws", [P, NU, SCALE5 * SCALE5])
        pw4 = sb("pw4", [P, NU * 4, 32])
        dw4 = sb("dw4", [P, NU * 4, DY_PE])
        w4 = sb("w4", [P, NU * 4, DY_PE, 32])
        ident = sb("ident1", [P, P])
        mask8 = sb("mask8", [P, P])
        headsel = sb("headsel", [P, 32])
        spread = sb("spread", [P, 4, P])
        qpad = sb("qpad", [P, 2, HP * WP + NSH])
        rep = sb("rep", [P, 2, 4, RROWS * WP])
        acc = sb("acc", [P, 2, HW])
        kva = sb("kva", [P, 2, HW])
        q = sb("q", [P, 4, HW])
        kT = sb("kT", [P, 2, 2, P])
        vT = sb("vT1", [P, 2, 2, P + 1])
        vkraw = sb("vkraw", [P, 2, P + 1])
        vkm = sb("vkm", [P, 2, P])
        vkmT = sb("vkmT", [P, 2, P])
        dsel = sb("dsel", [P, 4, 32])
        mt = sb("mt1", [P, 4, C])
        rcp = acc[:, 1]

        pj = ps("pj", [P, 2, 512])
        cv = ps("cv", [P, 2, 512])
        tr = ps("tr", [P, 2, 512])
        vk = ps("vk", [P, 512])
        ao = ps("ao", [P, 512])

        (w_in, x_in, zeroed, ones_set, w4_ready, pj_filled, pj_freed, rep_in0, rep_in1, tap_done,
         cv_filled, cv_freed, tr_filled, tr_freed, vk_step, vk_freed,
         vkm_ready, dsel_ready, sa_filled, sa_freed, sb_filled, sb_freed, den_filled, den_freed, r_ready,
         bc_filled, bc_freed, y_filled, y_freed, bn_done, y_out) = (
            sem(f"l1_{n}") for n in (
                "w_in x_in zeroed ones_set w4_ready pj_filled pj_freed rep_in0 rep_in1 tap_done "
                "cv_filled cv_freed tr_filled tr_freed vk_step vk_freed "
                "vkm_ready dsel_ready sa_filled sa_freed sb_filled sb_freed den_filled den_freed r_ready "
                "bc_filled bc_freed y_filled y_freed bn_done y_out").split())
        rep_in = (rep_in0, rep_in1)
        NW = 10

        def padded(b):
            return qpad[:, b, 0:HP * WP].rearrange("p (r c) -> p r c", r=HP)

        def bc_bank(j):
            return (tr if j < 2 else cv)[:, j % 2]

        def unit_at(i, u):
            return (i, u) if u < NU else (i + 1, u - NU)

        block = ctx.enter_context(nc.Block())

        @block.sync
        def _(sp):
            sp.dma_start(x1[:], dram["x1"][0]).then_inc(x_in, 16)
            for dst, name in ((wqkv, "wqkv"), (wproj, "wproj"), (pwbd, "pwbd"), (dws, "dws"), (pw4, "pw4"),
                              (dw4, "dw4"), (ident, "ident"), (mask8, "mask8"), (headsel, "headsel"),
                              (spread, "spread")):
                sp.dma_start(dst[:], dram[name]).then_inc(w_in, 16)

            def image(i, nxt):
                for u in range(NU):
                    v_proj = settle(sp, i * (NU * NCH) + (u + 1) * NCH)
                    v_half = [settle(sp, (NU * i + u - 1) * NCH + 3 * (h + 1))
                              for h in range(2)]
                    if u == 3:
                        v_y = settle(sp, 2 * NCH * i)
                        at = settle(sp, i - 1)
                        if not isinstance(i, int) or i > 0:
                            sp.wait_ge(y_freed, v_y)
                            store_y(at)
                    if u == NU - 1 and nxt:
                        v_x = settle(sp, i * (NU * NCH) + NU * NCH)
                        at = settle(sp, i + 1)
                        sp.wait_ge(pj_filled, v_x)
                        sp.dma_start(x1[:], image_of(dram["x1"], at)).then_inc(x_in, 16)
                    sp.wait_ge(pj_freed, v_proj)
                    for h in range(2):
                        wait_count(sp, cv_filled, v_half[h])
                        for b in range(4):
                            for s in range(NSH):
                                first = h * HALF * WP + s
                                sp.dma_start(rep[32 * s:32 * s + 32, h, b, :],
                                             qpad[32 * b:32 * b + 32, u % 2, first:first + RROWS * WP]
                                             ).then_inc(rep_in[h], 16)

            def store_y(at):
                sp.dma_start(image_of(dram["y"], at), q[:, 0:2, :]).then_inc(y_out, 16)

            image(0, True)
            with sp.Fori(1, NIMG - 1) as i:
                image(i, True)
            image(NIMG - 1, False)
            sp.wait_ge(y_freed, 2 * NCH * NIMG)
            store_y(NIMG - 1)
            sp.wait_ge(y_out, 16 * NIMG)

        @block.tensor
        def _(pe):
            pe.wait_ge(w_in, 16 * NW)
            pe.wait_ge(w4_ready, 1)

            def project(i, u):
                if u == 0:
                    pe.wait_ge(x_in, 16 * i + 16)
                for c in range(NCH):
                    g = i * (NU * NCH) + u * NCH + c
                    wait_count(pe, pj_freed, g - 1)
                    for kc in range(CT):
                        mm = nc.tensor.matmul(pj[:, c % 2, :CHUNK], wqkv[:, kc, u, :],
                                              x1[:, kc, c * CHUNK:(c + 1) * CHUNK],
                                              start=(kc == 0), stop=(kc == CT - 1))
                    mm.then_inc(pj_filled, 1)

            def convolve(i, u):
                for c in range(NCH):
                    half, row = c // (NCH // 2), 8 * (c % (NCH // 2))
                    if c % (NCH // 2) == 0:
                        pe.wait_ge(rep_in[half], (i * NU + u + 1) * (16 * 16))
                    wait_count(pe, cv_freed, i * (NU * NCH) + u * NCH + c - 1)
                    if u == 0 and c == 0:
                        wait_count(pe, bc_freed, 4 * NCH * i)
                    if c == 0:
                        pe.wait_ge(tap_done, (i * NU + u + 1) * NT)
                    for b in range(4):
                        taps = rep[:, half, b, :].rearrange("p (r c) -> p r c", c=WP)
                        for dy in range(DY_PE):
                            nc.tensor.matmul(cv[32 * b:32 * b + 32, c % 2, :CHUNK], w4[:, 4 * u + b, dy, :],
                                             taps[:, row + dy:row + dy + 8, 0:W],
                                             start=(dy == 0), stop=False, skip_group_check=True)
                    mm = nc.tensor.matmul(cv[:, c % 2, :CHUNK], pwbd[:, u, :], acc[:, u % 2, c * CHUNK:(c + 1) * CHUNK],
                                          start=False, stop=True, skip_group_check=True)
                    mm.then_inc(cv_filled, 1)

            def product(i, p):
                u, source, half = PRODUCTS[p]
                groups = DG if source == 0 else AG
                base = i * NTR + SEG[p]

                def step(g):
                    pe.wait_ge(tr_freed, base + g + 1)
                    if g == 0:
                        wait_count(pe, vk_freed, i * 4 + p)
                        pe.wait_ge(ones_set, 1)
                    for t in range(2):
                        mm = nc.tensor.matmul(vk[:, 0:P + 1], kT[:, g % 2, t, :], vT[:, g % 2, t, :],
                                              start=(g == 0 and t == 0), stop=(g == groups - 1 and t == 1))
                    mm.then_inc(vk_step, 1)

                if source == 0:
                    pe.wait_ge(pj_freed, i * (NU * NCH) + (u + 2) * NCH)
                else:
                    pe.wait_ge(cv_freed, i * (NU * NCH) + (u + 2) * NCH)
                for g in range(groups):
                    wait_count(pe, tr_freed, base + (g - 1 if g >= 2 else 0))
                    if g == 0 and p:
                        wait_count(pe, y_freed, 2 * NCH * i)
                    for t in range(2):
                        for kv in range(2):
                            if source == 0:
                                first = DFIRST + (2 * g + t) * P
                                src = qpad[:, kv, first:first + P]
                            else:
                                src = kva[:, kv, (2 * g + t) * P:(2 * g + t + 1) * P]
                            mm = nc.tensor.transpose(tr[:, g % 2, (2 * kv + t) * P:(2 * kv + t + 1) * P], src, ident[:])
                    mm.then_inc(tr_filled, 1)
                    if g >= 1:
                        step(g - 1)
                step(groups - 1)

            def turn_product(i, p):
                pe.wait_ge(vkm_ready, 4 * i + p + 1)
                wait_count(pe, sb_freed, 4 * i + p)
                nc.tensor.transpose(ao[:, 0:P], vkm[:, p % 2, :], ident[:]).then_inc(sa_filled, 1)

            def project_product(i, p):
                pe.wait_ge(sa_freed, 4 * i + p + 1)
                nc.tensor.matmul(ao[:, P:P + C], vkmT[:, p % 2, :], wproj[:, slot_of(p), :],
                                 start=True, stop=True, skip_group_check=True).then_inc(sb_filled, 1)

            def denominators(i, c):
                if c == 0:
                    pe.wait_ge(sb_freed, 4 * i + 4)
                    pe.wait_ge(dsel_ready, 4 * i + 4)
                    pe.wait_ge(cv_freed, (i + 1) * NU * NCH)
                else:
                    pe.wait_ge(den_freed, i * NCH + c)
                for j in range(4):
                    mm = nc.tensor.matmul(ao[32 * j:32 * j + 32, 0:CHUNK], dsel[:, j, :],
                                          q[:, j, c * CHUNK:(c + 1) * CHUNK], start=True, stop=True, skip_group_check=True)
                mm.then_inc(den_filled, 1)

            def attend(i):
                denominators(i, 0)
                for c in range(NCH):
                    if c + 1 < NCH:
                        denominators(i, c + 1)
                    pe.wait_ge(r_ready, i * NCH + c + 1)
                    for j in range(4):
                        k = 4 * c + j
                        if c >= 1:
                            pe.wait_ge(bc_freed, 4 * NCH * i + k - 3)
                        nc.tensor.matmul(bc_bank(j)[:, :CHUNK], spread[:, j, :], rcp[:, c * CHUNK:(c + 1) * CHUNK],
                                         start=True, stop=True).then_inc(bc_filled, 1)

            def output(i):
                pe.wait_ge(bc_freed, 4 * NCH * (i + 1))
                for c in range(NCH):
                    for m in range(CT):
                        k = 2 * c + m
                        if k >= 2:
                            pe.wait_ge(y_freed, 2 * NCH * i + k - 1)
                        for j in range(4):
                            mm = nc.tensor.matmul(tr[:, k % 2, :CHUNK], mt[:, j, m * P:(m + 1) * P],
                                                  q[:, j, c * CHUNK:(c + 1) * CHUNK], start=(j == 0), stop=(j == 3))
                        mm.then_inc(y_filled, 1)

            def image(i, prev, nxt):
                for u in range(NU):
                    if u == 0:
                        product(i, 0)
                        if prev:
                            attend(i - 1)
                    if u == 2:
                        product(i, 2)
                    if u == 3:
                        turn_product(i, 2)
                    if u == 2:
                        turn_product(i, 1)
                    convolve(i, u)
                    if u + 2 < NU or nxt:
                        project(*unit_at(i, u + 2))
                    if u == 0 and prev:
                        output(i - 1)
                    if u == 0:
                        turn_product(i, 0)
                        project_product(i, 0)
                    if u == 1:
                        product(i, 1)
                    if u == 2:
                        project_product(i, 1)
                    if u == 3:
                        project_product(i, 2)
                        product(i, 3)
                    if u == 4:
                        turn_product(i, 3)
                    if u == 5:
                        project_product(i, 3)

            project(0, 0)
            project(0, 1)
            image(0, False, True)
            with pe.Fori(1, NIMG - 1) as i:
                image(i, True, True)
            image(NIMG - 1, True, False)
            attend(NIMG - 1)
            output(NIMG - 1)

        @block.scalar
        def _(act):
            act.wait_ge(zeroed, 1)

            def project(i, u):
                if not (isinstance(i, int) and i == 0 and u < 2):
                    act.wait_ge(tap_done, (i * NU + u - 1) * NT)
                    for h in range(2):
                        act.wait_ge(rep_in[h], (i * NU + u - 1) * 256)
                    if u in (0, 1):
                        act.wait_ge(tr_filled, i * NTR)
                    if u in (2, 3):
                        act.wait_ge(tr_filled, i * NTR + DG)
                    if u in (4, 5):
                        act.wait_ge(tr_filled, i * NTR + SEG[3])
                        if not (isinstance(i, int) and i == 0):
                            act.wait_ge(y_filled, 2 * NCH * i)
                        wait_count(act, bn_done, 2 * NCH * i)
                        wait_count(act, y_out, 16 * i)
                for c in range(NCH):
                    act.wait_ge(pj_filled, i * (NU * NCH) + u * NCH + c + 1)
                    src = pj[:, c % 2, :CHUNK]
                    if PARTS[u] == 0:
                        nc.scalar.activation(q[:, HALVES[u], c * CHUNK:(c + 1) * CHUNK], src, ACT.Relu)
                    dst = padded(u % 2)[:, PAD + 8 * c:PAD + 8 * c + 8, PAD:PAD + W]
                    nc.scalar.copy(dst, src.rearrange("p (r c) -> p r c", c=W)).then_inc(pj_freed, 1)

            def convolve(i, u):
                if u < 4:
                    wait_count(act, tr_filled, i * NTR + (SEG[2] if u >= 2 else 0))
                elif not (isinstance(i, int) and i == 0):
                    act.wait_ge(y_filled, 2 * NCH * i)
                for c in range(NCH):
                    act.wait_ge(cv_filled, i * (NU * NCH) + u * NCH + c + 1)
                    span = slice(c * CHUNK, (c + 1) * CHUNK)
                    if PARTS[u] == 0:
                        dst = q[:, 2 + HALVES[u], span]
                    else:
                        dst = kva[:, PARTS[u] - 1, span]
                    nc.scalar.activation(dst, cv[:, c % 2, :CHUNK], ACT.Copy if PARTS[u] == 2 else ACT.Relu
                                         ).then_inc(cv_freed, 1)

            def product(i, p):
                _, source, _ = PRODUCTS[p]
                groups = DG if source == 0 else AG
                base = i * NTR + SEG[p]
                for g in range(groups):
                    act.wait_ge(tr_filled, base + g + 1)
                    wait_count(act, vk_step, base + (g - 1 if g >= 2 else 0))
                    bank = tr[:, g % 2, :].rearrange("p (x t c) -> p x t c", x=2, t=2)
                    nc.scalar.activation(kT[:, g % 2], bank[:, 0], ACT.Relu)
                    nc.scalar.copy(vT[:, g % 2, :, 0:P], bank[:, 1]).then_inc(tr_freed, 1)
                act.wait_ge(vk_step, base + groups)
                wait_count(act, dsel_ready, 4 * i + p - 1)
                nc.scalar.copy(vkraw[:, p % 2, :], vk[:, 0:P + 1]).then_inc(vk_freed, 1)

            def turn_product(i, p):
                act.wait_ge(sa_filled, 4 * i + p + 1)
                nc.scalar.copy(vkmT[:, p % 2, :], ao[:, 0:P]).then_inc(sa_freed, 1)

            def project_product(i, p):
                act.wait_ge(sb_filled, 4 * i + p + 1)
                if not (isinstance(i, int) and i == 0):
                    act.wait_ge(y_filled, 2 * NCH * i)
                nc.scalar.copy(mt[:, slot_of(p), :], ao[:, P:P + C]).then_inc(sb_freed, 1)

            def output(i):
                for c in range(NCH):
                    for m in range(CT):
                        act.wait_ge(y_filled, 2 * NCH * i + 2 * c + 1 + m)
                        if m == 0:
                            continue
                        for mm_ in range(CT):
                            nc.scalar.copy(q[:, mm_, c * CHUNK:(c + 1) * CHUNK], tr[:, (2 * c + mm_) % 2, :CHUNK]
                                           ).then_inc(y_freed, 1)

            def image(i, prev, nxt):
                for u in range(NU):
                    if u == 0:
                        product(i, 0)
                    if u == 2:
                        product(i, 2)
                    if u == 3:
                        turn_product(i, 2)
                    if u == 2:
                        turn_product(i, 1)
                    convolve(i, u)
                    if u + 2 < NU or nxt:
                        project(*unit_at(i, u + 2))
                    if u == 0 and prev:
                        output(i - 1)
                    if u == 0:
                        turn_product(i, 0)
                        project_product(i, 0)
                    if u == 1:
                        product(i, 1)
                    if u == 2:
                        project_product(i, 1)
                    if u == 3:
                        project_product(i, 2)
                        product(i, 3)
                    if u == 4:
                        turn_product(i, 3)
                    if u == 5:
                        project_product(i, 3)

            project(0, 0)
            project(0, 1)
            image(0, False, True)
            with act.Fori(1, NIMG - 1) as i:
                image(i, True, True)
            image(NIMG - 1, True, False)
            output(NIMG - 1)

        @block.gpsimd
        def _(pool):
            nc.gpsimd.memset(qpad[:], 0.0).then_inc(zeroed, 1)
            nc.gpsimd.memset(vT[:, :, :, P:P + 1], 1.0).then_inc(ones_set, 1)
            pool.wait_ge(w_in, 16 * NW)

            def image(i):
                for p in range(4):
                    pool.wait_ge(vk_freed, 4 * i + p + 1)
                    if p >= 2:
                        pool.wait_ge(sa_filled, 4 * i + p - 1)
                    else:
                        wait_count(pool, sa_filled, 4 * i)
                    nc.gpsimd.tensor_tensor(vkm[:, p % 2, :], vkraw[:, p % 2, 0:P], mask8[:], ALU.mult).then_inc(vkm_ready, 1)
                    wait_count(pool, den_filled, NCH * i)
                    nc.gpsimd.tensor_tensor(dsel[:, slot_of(p), :], headsel[:],
                                            vkraw[:, p % 2, P:P + 1].to_broadcast([P, 32]), ALU.mult
                                            ).then_inc(dsel_ready, 1)

            image(0)
            with pool.Fori(1, NIMG) as i:
                image(i)

        @block.vector
        def _(dve):
            dve.wait_ge(w_in, 16 * NW)
            nc.vector.tensor_tensor(w4[:], pw4[:].rearrange("p b (o c) -> p b o c", o=1).to_broadcast([P, NU * 4, DY_PE, 32]),
                                    dw4[:].rearrange("p b (r o) -> p b r o", o=1).to_broadcast([P, NU * 4, DY_PE, 32]),
                                    ALU.mult).then_inc(w4_ready, 1)

            def taps(i, u):
                dve.wait_ge(pj_freed, i * (NU * NCH) + (u + 1) * NCH)
                wait_count(dve, cv_filled, (i * NU + u - 1) * NCH)
                a = acc[:, u % 2].rearrange("p (r c) -> p r c", c=W)
                for k, (dy, dx) in enumerate(DVE_TAPS):
                    src = padded(u % 2)[:, dy:dy + H, dx:dx + W]
                    w = dws[:, u, SCALE5 * dy + dx:SCALE5 * dy + dx + 1]
                    if k == 0:
                        op = nc.vector.tensor_scalar(a, src, w, None, ALU.mult)
                    else:
                        dve.wait_ge(tap_done, (i * NU + u) * NT + k)
                        op = nc.vector.scalar_tensor_tensor(out=a, in0=src, scalar=w, in1=a, op0=ALU.mult, op1=ALU.add)
                    op.then_inc(tap_done, 1)

            def reciprocals(i, c):
                dve.wait_ge(den_filled, i * NCH + c + 1)
                r = rcp[:, c * CHUNK:(c + 1) * CHUNK]
                nc.vector.tensor_scalar(r, ao[:, 0:CHUNK], EPS_ATT, None, ALU.add).then_inc(den_freed, 1)
                dve.wait_ge(den_freed, i * NCH + c + 1)
                nc.vector.reciprocal(r, r).then_inc(r_ready, 1)

            def attend(i):
                reciprocals(i, 0)
                for c in range(NCH):
                    if c + 1 < NCH:
                        reciprocals(i, c + 1)
                    for j in range(4):
                        k = 4 * c + j
                        dve.wait_ge(bc_filled, 4 * NCH * i + k + 1)
                        qc = q[:, j, c * CHUNK:(c + 1) * CHUNK]
                        nc.vector.tensor_tensor(qc, qc, bc_bank(j)[:, :CHUNK], ALU.mult).then_inc(bc_freed, 1)

            def statistics(i):
                for c in range(NCH):
                    for m in range(CT):
                        dve.wait_ge(y_freed, 2 * NCH * i + 2 * c + m + 1)
                        nc.vector.bn_stats(bnst_at(i, m, c), q[:, m, c * CHUNK:(c + 1) * CHUNK]).then_inc(bn_done, 1)

            def bnst_at(i, m, c):
                if isinstance(i, int):
                    return bnst[:, m, i, c, :]
                return bnst[:, m, bass.ds(i, 1), c, :].rearrange("p o s -> p (o s)")

            def image(i, prev):
                taps(i, 0)
                if prev:
                    attend(i - 1)
                taps(i, 1)
                taps(i, 2)
                if prev:
                    statistics(i - 1)
                for u in range(3, NU):
                    taps(i, u)

            image(0, False)
            with dve.Fori(1, NIMG) as i:
                image(i, True)
            attend(NIMG - 1)
            statistics(NIMG - 1)


def phase_out(nc, dram, sem, bnst):
    with ExitStack() as ctx:
        def sb(name, shape):
            return ctx.enter_context(nc.sbuf_tensor(name, shape, F32))

        RING = 4
        yb = sb("yb", [P, RING, CT, HW])
        xb = sb("xb", [P, RING, CT, HW])
        gb = sb("gb", [P, 2, CT])
        agg = sb("agg", [P, CT, 2])
        ve = sb("ve", [P, CT])
        rt = sb("rt", [P, CT])
        r0 = sb("r0", [P, CT])
        t0 = sb("t0", [P, CT])
        sc = sb("sc", [P, CT])
        sh = sb("sh", [P, CT])

        g_in, stat, root, load0, load1, load2, load3, scaled, summed, store0, store1, store2, store3 = (
            sem(f"out_{n}") for n in
            "g_in stat root load0 load1 load2 load3 scaled summed store0 store1 store2 store3".split())
        load, store = (load0, load1, load2, load3), (store0, store1, store2, store3)

        block = ctx.enter_context(nc.Block())

        @block.sync
        def _(sp):
            sp.dma_start(gb[:], dram["gb"]).then_inc(g_in, 16)
            for n in range(NIMG):
                r = n % RING
                if n >= RING:
                    sp.wait_ge(store[r], 16 * (n // RING))
                sp.dma_start(yb[:, r], dram["y"][n]).then_inc(load[r], 16)
                sp.dma_start(xb[:, r], dram["x1"][n]).then_inc(load[r], 16)

        @block.gpsimd
        def _(pool):
            for n in range(NIMG):
                r = n % RING
                pool.wait_ge(summed, n + 1)
                pool.dma_start(dram["out"][n], yb[:, r]).then_inc(store[r], 16)
            for r in range(RING):
                pool.wait_ge(store[r], 16 * (NIMG // RING))

        @block.scalar
        def _(act):
            act.wait_ge(stat, CT + 1)
            nc.scalar.activation(rt[:], ve[:], ACT.Sqrt).then_inc(root, 1)
            act.wait_ge(stat, CT + 9)
            for n in range(NIMG):
                r = n % RING
                act.wait_ge(load[r], 32 * (n // RING + 1))
                for m in range(CT):
                    last = nc.scalar.activation(yb[:, r, m], yb[:, r, m], ACT.Identity, bias=sh[:, m:m + 1], scale=sc[:, m:m + 1])
                last.then_inc(scaled, 1)

        @block.vector
        def _(dve):
            done = [0]

            def step(op):
                done[0] += 1
                op.then_inc(stat, 1)
                dve.wait_ge(stat, done[0])

            for m in range(CT):
                step(nc.vector.bn_aggr(agg[:, m], bnst[:, m].rearrange("p i c s -> p (i c s)")))
            step(nc.vector.tensor_scalar(ve[:], agg[:, :, 1], EPS_BN, None, ALU.add))
            dve.wait_ge(root, 1)
            dve.wait_ge(g_in, 16)
            step(nc.vector.reciprocal(r0[:], rt[:]))
            step(nc.vector.tensor_tensor(t0[:], r0[:], r0[:], ALU.mult))
            step(nc.vector.tensor_tensor(t0[:], t0[:], ve[:], ALU.mult))
            step(nc.vector.tensor_scalar(t0[:], t0[:], -0.5, 1.5, ALU.mult, ALU.add))
            step(nc.vector.tensor_tensor(r0[:], r0[:], t0[:], ALU.mult))
            step(nc.vector.tensor_tensor(sc[:], r0[:], gb[:, 0], ALU.mult))
            step(nc.vector.tensor_tensor(t0[:], agg[:, :, 0], sc[:], ALU.mult))
            nc.vector.tensor_tensor(sh[:], gb[:, 1], t0[:], ALU.subtract).then_inc(stat, 1)
            for n in range(NIMG):
                r = n % RING
                dve.wait_ge(scaled, n + 1)
                nc.vector.tensor_tensor(yb[:, r], yb[:, r], xb[:, r], ALU.add).then_inc(summed, 1)


def build(nc, dram):
    with ExitStack() as ctx:
        def sem(name):
            return ctx.enter_context(nc.semaphore(name))

        bnst = ctx.enter_context(nc.sbuf_tensor("bnst", [P, CT, NIMG, NCH, 6], F32))
        phase_l0(nc, dram, sem)
        phase_l1(nc, dram, sem, bnst)
        phase_out(nc, dram, sem, bnst)


def layouts(inputs):
    import numpy as np

    a = {n: np.ascontiguousarray(v) for n, v in inputs.items()}

    def columns(v, parts):
        return v.reshape(parts, P).T

    out = {}
    out["x"] = a["x"].reshape(NIMG, CT, P, HW).transpose(0, 2, 1, 3)
    out["wk"] = a["L0_conv_Wk"].T.reshape(CT, P, C).transpose(1, 0, 2)
    out["wqv"] = np.concatenate([a["L0_conv_Wq"].T, a["L0_conv_Wv"].T], 1).reshape(CT, P, 2 * C).transpose(1, 0, 2)
    out["wp"] = a["L0_conv_Wp"].T.reshape(CT, P, C).transpose(1, 0, 2)
    out["bqv"] = np.broadcast_to(np.stack([a["L0_conv_bq"], a["L0_conv_bv"]]), (P, 2, C))
    out["bkp"] = np.stack([columns(a["L0_conv_bk"], CT), columns(a["L0_conv_bp"], CT)], 1)

    rows = np.array([[3 * DIM * h + DIM * PARTS[u] + d for h in range(16 * HALVES[u], 16 * HALVES[u] + 16)
                      for d in range(DIM)] for u in range(NU)])
    wq = a["L1_conv_w_qkv"][rows]
    out["wqkv"] = wq.transpose(2, 0, 1).reshape(CT, P, NU, P).transpose(1, 0, 2, 3)
    out["wproj"] = a["L1_conv_w_proj"].T.reshape(4, P, C).transpose(1, 0, 2)
    pw = a["L1_conv_w_pw"][rows[:, ::DIM] // DIM]
    bd = np.zeros((NU, P, P), pw.dtype)
    for g in range(16):
        bd[:, 8 * g:8 * g + 8, 8 * g:8 * g + 8] = pw[:, g].transpose(0, 2, 1)
    out["pwbd"] = bd.transpose(1, 0, 2)
    blocks = np.stack([bd[:, 32 * b:32 * b + 32, 32 * b:32 * b + 32] for b in range(4)], 1)
    out["pw4"] = np.tile(blocks.reshape(NU * 4, 32, 32).transpose(1, 0, 2), (NSH, 1, 1))
    dw = a["L1_conv_w_dw"].reshape(-1, SCALE5, SCALE5)[rows]
    out["dws"] = dw.reshape(NU, P, SCALE5 * SCALE5).transpose(1, 0, 2)
    stack = dw[:, :, :DY_PE, :NSH].reshape(NU, 4, 32, DY_PE, NSH)
    out["dw4"] = stack.transpose(4, 2, 0, 1, 3).reshape(P, NU * 4, DY_PE)
    out["gb"] = np.stack([columns(a["L1_conv_bn_gamma"], CT), columns(a["L1_conv_bn_beta"], CT)], 1)

    k = np.arange(P)
    out["ident"] = np.eye(P, dtype=np.float32)
    out["mask32"] = (k[:, None] // HD0 == k[None] // HD0).astype(np.float32)
    out["mask8"] = (k[:, None] // DIM == k[None] // DIM).astype(np.float32)
    out["headsel"] = (k[:, None] // DIM == np.arange(32)[None] % 16).astype(np.float32)
    j = np.arange(4)
    out["spread"] = ((k[:, None, None] // 32 == j[None, :, None]) & (k[:, None, None] % 32 == k[None, None] // DIM)
                     ).astype(np.float32)
    return {n: np.ascontiguousarray(v) for n, v in out.items()}


def kernel(**inputs):
    import numpy as _np
    import concourse.bacc as _bacc
    from concourse.bass_utils import run_bass_kernel_spmd as _run

    nc = _bacc.Bacc("TRN2", target_bir_lowering=False, num_devices=1)
    arrays, dram = {}, {}
    for name, a in layouts(inputs).items():
        arrays[f"in_{name}"] = a
        dram[name] = nc.dram_tensor(f"in_{name}", a.shape, mybir.dt.from_np(a.dtype), kind="ExternalInput").ap()
    for name in ("x1", "y"):
        dram[name] = nc.dram_tensor(f"scratch_{name}", (NIMG, P, CT, HW), F32).ap()
    dram["out"] = nc.dram_tensor("out_0", (NIMG, P, CT, HW), F32, kind="ExternalOutput").ap()
    build(nc, dram)
    r = _run(nc, [arrays], core_ids=[0])
    got = r.results[0]["out_0"]
    return _np.ascontiguousarray(got.transpose(0, 2, 1, 3)).reshape(NIMG, C, H, W)
```

```python
from contextlib import ExitStack

import concourse.bass as bass
from concourse import mybir
from concourse.alu_op_type import AluOpType as ALU

ACT = mybir.ActivationFunctionType
F32 = mybir.dt.float32
F32R = mybir.dt.float32r
AX = mybir.AxisListType

P = 128
NIMG, C, H, W = 8, 256, 48, 48
HW = H * W
CT = C // P
CHUNK = 8 * W
NCH = HW // CHUNK

HEADS0, HD0 = 8, 32
PAIR = 2 * P
NPAIR = HW // PAIR

DIM, SCALE5, PAD = 8, 5, 2
HP, WP = H + 2 * PAD, W + 2 * PAD
NU = 6
PARTS = (1, 2, 1, 2, 0, 0)
HALVES = (0, 0, 1, 1, 0, 1)
EPS_ATT, EPS_BN = 1e-15, 1e-5
DY_PE = 3
NSH = 4
HALF = H // 2
RROWS = HALF + DY_PE - 1
DVE_TAPS = [(dy, dx) for dy in range(SCALE5) for dx in range(SCALE5) if not (dy < DY_PE and dx < NSH)]
NT = len(DVE_TAPS)
DG, AG = 10, HW // (2 * P)
DFIRST = PAD * WP - (DG * 2 * P - H * WP) // 2
assert DFIRST >= 0 and DFIRST + DG * 2 * P <= HP * WP and DFIRST + DG * 2 * P >= (PAD + H) * WP
PRODUCTS = ((0, 0, 0), (0, 1, 0), (2, 0, 1), (2, 1, 1))
SEG = (0, DG, DG + AG, 2 * DG + AG)
NTR = 2 * (DG + AG)


def slot_of(product):
    _, source, half = PRODUCTS[product]
    return 2 * source + half


def wait_count(eng, sem, value):
    if isinstance(value, int) and value <= 0:
        return
    eng.wait_ge(sem, value)


def settle(eng, value):
    return value if isinstance(value, int) else eng.snap(value)


def image_of(array, i):
    return array[i] if isinstance(i, int) else array[bass.ds(i, 1)].rearrange("o p c t -> p (o c) t")


def phase_l0(nc, dram, sem):
    with ExitStack() as ctx:
        def sb(name, shape, dtype=F32):
            return ctx.enter_context(nc.sbuf_tensor(name, shape, dtype))

        def ps(name, shape):
            return ctx.enter_context(nc.psum_tensor(name, shape, F32))

        xs = sb("xs", [P, 2, CT, HW])
        xhi = sb("xhi", [P, 2, CT, HW], F32R)
        xlo = sb("xlo", [P, 2, CT, HW], F32R)
        wkqv = sb("wkqv", [P, CT, 3 * C])
        whi = sb("whi", [P, CT, 3 * C], F32R)
        wlo = sb("wlo", [P, CT, 3 * C], F32R)
        wp = sb("wp", [P, CT, C])
        bqv = sb("bqv", [P, 2, C])
        bkp = sb("bkp", [P, 2, CT])
        ident = sb("ident0", [P, P])
        mask32 = sb("mask32", [P, P])
        keys = sb("keys", [P, CT, HW])
        nmax = sb("nmax", [P, CT])
        ksum = sb("ksum", [P, CT])
        rk = sb("rk", [P, CT])
        vT = sb("vT", [P, HW // P, C])
        ekT = sb("ekT", [P, 2, 2, C])
        ctxm = sb("ctxm", [P, CT, P])
        mt = sb("mt", [P, CT, C])
        qs = sb("qs", [P, NPAIR, 2, HEADS0, HD0])
        qmx = sb("qmx", [P, 2, 2 * HEADS0])
        qsm = sb("qsm", [P, 2, 2 * HEADS0])
        qrc = sb("qrc", [P, 2, 2 * HEADS0])
        mthi = sb("mthi", [P, CT, C], F32R)
        mtlo = sb("mtlo", [P, CT, C], F32R)
        qnhi = sb("qnhi", [P, 2, CT, PAIR], F32R)
        qnlo = sb("qnlo", [P, 2, CT, PAIR], F32R)

        kx = ps("kx", [P, 2, 512])
        qv = ps("qv", [P, 4, 512])
        ep = ps("ep", [P, 2, 512])

        def ebank(n):
            return ep[:, n % 2, :].rearrange("p (t c) -> p t c", t=2)

        (w_in, w_hi, w_lo, x_in0, x_in1, x_out0, x_out1, hi_ready, lo_ready, k_filled, k_freed, nmax_ready, exp_done,
         qv_filled, v_done, q_added, e_filled, e_freed, ctx_step, ctx_masked, rk_ready, m_filled, mt_ready, mthi_ready, mtlo_ready, qnlo_ready, q_maxed,
         q_shifted, q_exp, q_summed, q_recip, q_ready, x_filled, x1_done) = (
            sem(f"l0_{n}") for n in (
                "w_in w_hi w_lo x_in0 x_in1 x_out0 x_out1 hi_ready lo_ready k_filled k_freed nmax_ready exp_done "
                "qv_filled v_done q_added e_filled e_freed ctx_step ctx_masked rk_ready m_filled mt_ready mthi_ready mtlo_ready qnlo_ready q_maxed "
                "q_shifted q_exp q_summed q_recip q_ready x_filled x1_done").split())
        x_in, x_out = (x_in0, x_in1), (x_out0, x_out1)
        NW = 6
        NE = 2 * NPAIR
        NK = CT * NCH
        PIECES = 4
        PIECE = HW // PIECES

        def piece(array, par, s):
            return array[:, par, :, s * PIECE:(s + 1) * PIECE]

        def split_input(eng, par, it):
            eng.wait_ge(x_in[1 - par], (it + 1 + par) * 16)
            return 1 - par

        block = ctx.enter_context(nc.Block())

        @block.sync
        def _(sp):
            for par in range(2):
                sp.dma_start(xs[:, par], dram["x"][par]).then_inc(x_in[par], 16)
                if par == 0:
                    for dst, name in ((wkqv, "wkqv"), (wp, "wp"), (bqv, "bqv"), (bkp, "bkp"),
                                      (ident, "ident"), (mask32, "mask32")):
                        sp.dma_start(dst[:], dram[name]).then_inc(w_in, 16)
            with sp.Fori(0, NIMG // 2 - 1) as it:
                for par in range(2):
                    written = sp.snap((2 * it + par + 1) * NPAIR)
                    stored = sp.snap((it + 1) * 16)
                    here = sp.snap(2 * it + par)
                    there = sp.snap(2 * it + par + 2)
                    sp.wait_ge(x1_done, written)
                    sp.dma_start(image_of(dram["x1"], here),
                                 xs[:, par]).then_inc(x_out[par], 16)
                    sp.wait_ge(x_out[par], stored)
                    sp.dma_start(xs[:, par], image_of(dram["x"], there)).then_inc(x_in[par], 16)
            for par in range(2):
                n = NIMG - 2 + par
                sp.wait_ge(x1_done, (n + 1) * NPAIR)
                sp.dma_start(dram["x1"][n], xs[:, par]).then_inc(x_out[par], 16)
            for par in range(2):
                sp.wait_ge(x_out[par], 16 * NIMG // 2)

        @block.tensor
        def _(pe):
            pe.wait_ge(w_in, 16 * NW)
            pe.wait_ge(w_hi, 1)
            pe.wait_ge(w_lo, 1)

            def product3(out, left, right, start, stop):
                (lhi, llo), (rhi, rlo) = left, right
                nc.tensor.matmul(out, lhi, rhi, start=start, stop=False, skip_group_check=True)
                nc.tensor.matmul(out, lhi, rlo, start=False, stop=False, skip_group_check=True)
                return nc.tensor.matmul(out, llo, rhi, start=False, stop=stop, skip_group_check=True)

            def image(n, par):
                def x_part(kc, first, size):
                    return tuple(x[:, par, kc, first:first + size] for x in (xhi, xlo))

                def w_part(kc, first, size):
                    return tuple(w[:, kc, first:first + size] for w in (whi, wlo))

                def key_group(g):
                    m, c = g // NCH, g % NCH
                    if g < 2:
                        wait_count(pe, x1_done, n * NPAIR - 1 + g)
                    else:
                        pe.wait_ge(k_freed, n * NK + g - 1)
                    for kc in range(CT):
                        mm = product3(kx[:, (g + 1) % 2, :CHUNK], w_part(kc, m * P, P), x_part(kc, c * CHUNK, CHUNK),
                                      kc == 0, kc == CT - 1)
                    mm.then_inc(k_filled, 1)

                def token_major(g):
                    wait_count(pe, v_done, n * NPAIR + g - 1)
                    wait_count(pe, q_added, n * NPAIR + g - 1)
                    for t in range(2):
                        for kc in range(CT):
                            mm = product3(qv[:, 2 * (g % 2) + t, :], x_part(kc, (2 * g + t) * P, P),
                                          w_part(kc, C, 2 * C), kc == 0, kc == CT - 1)
                    mm.then_inc(qv_filled, 1)

                def turn_keys(g):
                    if g == 0:
                        pe.wait_ge(exp_done, (n + 1) * CT)
                    wait_count(pe, e_freed, n * NE + g - 1)
                    if g < 2:
                        wait_count(pe, qnlo_ready, n * NPAIR)
                    for t in range(2):
                        for h in range(CT):
                            mm = nc.tensor.transpose(ebank(g)[:, t, h * P:(h + 1) * P],
                                                     keys[:, h, (2 * g + t) * P:(2 * g + t + 1) * P], ident[:])
                    mm.then_inc(e_filled, 1)

                def context(g):
                    pe.wait_ge(e_freed, n * NE + g + 1)
                    pe.wait_ge(v_done, n * NPAIR + g + 1)
                    if g == 0:
                        pe.wait_ge(k_freed, (n + 1) * NK)
                    for t in range(2):
                        for h in range(CT):
                            mm = nc.tensor.matmul(kx[:, 0, h * P:(h + 1) * P],
                                                  vT[:, 2 * g + t, h * P:(h + 1) * P],
                                                  ekT[:, g % 2, t, h * P:(h + 1) * P],
                                                  start=(g == 0 and t == 0 and h == 0),
                                                  stop=(g == NPAIR - 1 and t == 1), skip_group_check=True)
                    mm.then_inc(ctx_step, 1)

                def turn_queries(g):
                    k = NPAIR + g
                    pe.wait_ge(q_ready, n * NPAIR + g + 1)
                    pe.wait_ge(e_freed, n * NE + k - 1)
                    if g >= 2:
                        pe.wait_ge(qnlo_ready, n * NPAIR + g - 1)
                    for t in range(2):
                        for h in range(CT):
                            src = qs[:, g, t, 4 * h:4 * h + 4, :].rearrange("p a b -> p (a b)")
                            mm = nc.tensor.transpose(ebank(k)[:, h, t * P:(t + 1) * P], src, ident[:])
                    mm.then_inc(e_filled, 1)

                def x1_group(g):
                    pe.wait_ge(e_freed, n * NE + NPAIR + g + 1)
                    pe.wait_ge(qnlo_ready, n * NPAIR + g + 1)
                    if g == 0:
                        pe.wait_ge(mthi_ready, n + 1)
                        pe.wait_ge(mtlo_ready, n + 1)
                    if g >= 2:
                        pe.wait_ge(x1_done, n * NPAIR + g - 1)
                    for m in range(CT):
                        for kc in range(CT):
                            mm = product3(kx[:, g % 2, m * PAIR:(m + 1) * PAIR],
                                          tuple(a[:, kc, m * P:(m + 1) * P] for a in (mthi, mtlo)),
                                          tuple(a[:, g % 2, kc, :] for a in (qnhi, qnlo)), kc == 0, kc == CT - 1)
                    mm.then_inc(x_filled, 1)

                pe.wait_ge(hi_ready, (n + 1) * PIECES)
                pe.wait_ge(lo_ready, (n + 1) * PIECES)
                for g in range(NK):
                    key_group(g)
                for g in range(NPAIR):
                    token_major(g)
                    if g >= 2:
                        turn_keys(g - 2)
                    if g >= 3:
                        context(g - 3)
                for g in range(NPAIR - 2, NPAIR):
                    turn_keys(g)
                    context(g - 1)
                context(NPAIR - 1)
                turn_queries(0)
                pe.wait_ge(ctx_masked, n + 1)
                for h in range(CT):
                    mm = nc.tensor.matmul(kx[:, 1, h * C:(h + 1) * C], ctxm[:, h], wp[:, h],
                                          start=True, stop=True, skip_group_check=True)
                mm.then_inc(m_filled, 1)
                for g in range(1, NPAIR):
                    turn_queries(g)
                    x1_group(g - 1)
                x1_group(NPAIR - 1)

            for par in range(2):
                image(par, par)
            with pe.Fori(1, NIMG // 2) as it:
                for par in range(2):
                    image(2 * it + par, par)

        @block.scalar
        def _(act):
            act.wait_ge(w_in, 16 * NW)
            nc.scalar.copy(whi[:], wkqv[:]).then_inc(w_hi, 1)

            def high(par, s):
                nc.scalar.copy(piece(xhi, par, s), piece(xs, par, s)).then_inc(hi_ready, 1)

            act.wait_ge(x_in[0], 16)
            for s in range(PIECES):
                high(0, s)

            def image(n, par, it, nxt):
                def exponentials(g):
                    act.wait_ge(e_filled, n * NE + g + 1)
                    wait_count(act, ctx_step, n * NPAIR + g - 1)
                    nc.scalar.copy(ekT[:, g % 2], ebank(g)).then_inc(e_freed, 1)

                def exp_q(g):
                    act.wait_ge(q_shifted, n * NPAIR + g + 1)
                    nc.scalar.activation(qs[:, g], qs[:, g], ACT.Exp).then_inc(q_exp, 1)

                wait_count(act, e_filled, n * NE)
                for g in range(NK):
                    m, c = g // NCH, g % NCH
                    act.wait_ge(k_filled, n * NK + g + 1)
                    nc.scalar.activation(keys[:, m, c * CHUNK:(c + 1) * CHUNK], kx[:, (g + 1) % 2, :CHUNK],
                                         ACT.Identity, bias=bkp[:, 0, m:m + 1]).then_inc(k_freed, 1)
                wait_count(act, rk_ready, n)
                for m in range(CT):
                    act.wait_ge(nmax_ready, n * CT + m + 1)
                    nc.scalar.activation(keys[:, m, :], keys[:, m, :], ACT.Exp, bias=nmax[:, m:m + 1],
                                         accum_out=ksum[:, m:m + 1]).then_inc(exp_done, 1)
                for g in range(NPAIR):
                    if g >= 2:
                        exponentials(g - 2)
                    exp_q(g)
                    if nxt and 5 <= g < 5 + PIECES:
                        if g == 5:
                            wait_count(act, qv_filled, n * NPAIR)
                        high(split_input(act, par, it), g - 5)
                for g in range(NPAIR - 2, NPAIR):
                    exponentials(g)
                act.wait_ge(m_filled, n + 1)
                act.wait_ge(rk_ready, n + 1)
                wait_count(act, mtlo_ready, n)
                wait_count(act, x_filled, n * NPAIR)
                for h in range(CT):
                    last = nc.scalar.activation(mt[:, h], kx[:, 1, h * C:(h + 1) * C], ACT.Copy, scale=rk[:, h:h + 1])
                last.then_inc(mt_ready, 1)
                act.wait_ge(mt_ready, n + 1)
                nc.scalar.copy(mthi[:], mt[:]).then_inc(mthi_ready, 1)
                for g in range(NPAIR):
                    act.wait_ge(e_filled, n * NE + NPAIR + g + 1)
                    wait_count(act, x_filled, n * NPAIR + (g - 1 if g >= 2 else 0))
                    nc.scalar.copy(qnhi[:, g % 2], ebank(NPAIR + g)).then_inc(e_freed, 1)

            for par in range(2):
                image(par, par, 0, True)
            with act.Fori(1, NIMG // 2 - 1) as it:
                for par in range(2):
                    image(2 * it + par, par, it, True)
            for par in range(2):
                image(NIMG - 2 + par, par, NIMG // 2 - 1, par == 0)

        @block.gpsimd
        def _(pool):
            def image(n):
                for g in range(NPAIR):
                    pool.wait_ge(q_recip, n * NPAIR + g + 1)
                    qh = qs[:, g].rearrange("p t h d -> p (t h) d")
                    nc.gpsimd.tensor_tensor(qh, qh, qrc[:, g % 2].rearrange("p (h o) -> p h o", o=1).to_broadcast(
                        [P, 2 * HEADS0, HD0]), ALU.mult).then_inc(q_ready, 1)

            image(0)
            with pool.Fori(1, NIMG) as n:
                image(n)

        @block.vector
        def _(dve):
            dve.wait_ge(w_in, 16 * NW)
            dve.wait_ge(w_hi, 1)
            nc.vector.tensor_tensor(wlo[:], wkqv[:], whi[:].bitcast(F32), ALU.subtract).then_inc(w_lo, 1)

            def low(n, par, s):
                dve.wait_ge(hi_ready, n * PIECES + s + 1)
                nc.vector.tensor_tensor(piece(xlo, par, s), piece(xs, par, s), piece(xhi, par, s).bitcast(F32),
                                        ALU.subtract).then_inc(lo_ready, 1)

            for s in range(PIECES):
                low(0, 0, s)

            def image(n, par, nxt):
                def values(g):
                    dve.wait_ge(qv_filled, n * NPAIR + g + 1)
                    if g == 0:
                        wait_count(dve, ctx_step, n * NPAIR)
                    nc.vector.tensor_tensor(vT[:, 2 * g:2 * g + 2, :], qv[:, 2 * (g % 2):2 * (g % 2) + 2, C:2 * C],
                                            bqv[:, 1:2, :].to_broadcast([P, 2, C]), ALU.add).then_inc(v_done, 1)

                def shift_q(g):
                    if g == 0:
                        wait_count(dve, e_filled, n * NE)
                    q = qs[:, g].rearrange("p t h d -> p t (h d)")
                    qh = qs[:, g].rearrange("p t h d -> p (t h) d")
                    nc.vector.tensor_tensor(q, qv[:, 2 * (g % 2):2 * (g % 2) + 2, 0:C],
                                            bqv[:, 0:1, :].to_broadcast([P, 2, C]), ALU.add).then_inc(q_added, 1)
                    dve.wait_ge(q_added, n * NPAIR + g + 1)
                    nc.vector.tensor_reduce(qmx[:, g % 2], qh, AX.X, ALU.max).then_inc(q_maxed, 1)
                    dve.wait_ge(q_maxed, n * NPAIR + g + 1)
                    nc.vector.tensor_tensor(qh, qh, qmx[:, g % 2].rearrange("p (h o) -> p h o", o=1).to_broadcast(
                        [P, 2 * HEADS0, HD0]), ALU.subtract).then_inc(q_shifted, 1)

                def sum_q(g):
                    qh = qs[:, g].rearrange("p t h d -> p (t h) d")
                    dve.wait_ge(q_exp, n * NPAIR + g + 1)
                    nc.vector.tensor_reduce(qsm[:, g % 2], qh, AX.X, ALU.add).then_inc(q_summed, 1)
                    dve.wait_ge(q_summed, n * NPAIR + g + 1)
                    wait_count(dve, q_ready, n * NPAIR + g - 1)
                    nc.vector.reciprocal(qrc[:, g % 2], qsm[:, g % 2]).then_inc(q_recip, 1)

                def low_q(g):
                    dve.wait_ge(e_freed, n * NE + NPAIR + g + 1)
                    wait_count(dve, x_filled, n * NPAIR + (g - 1 if g >= 2 else 0))
                    nc.vector.tensor_tensor(qnlo[:, g % 2], ebank(NPAIR + g), qnhi[:, g % 2].bitcast(F32),
                                            ALU.subtract).then_inc(qnlo_ready, 1)

                def add_x(g):
                    dve.wait_ge(x_filled, n * NPAIR + g + 1)
                    for m in range(CT):
                        xt = xs[:, par, m, g * PAIR:(g + 1) * PAIR]
                        last = nc.vector.scalar_tensor_tensor(out=xt, in0=kx[:, g % 2, m * PAIR:(m + 1) * PAIR],
                                                              scalar=bkp[:, 1, m:m + 1], in1=xt,
                                                              op0=ALU.add, op1=ALU.add)
                    last.then_inc(x1_done, 1)

                wait_count(dve, exp_done, n * CT)
                for m in range(CT):
                    dve.wait_ge(k_freed, n * NK + (m + 1) * NCH)
                    nc.vector.tensor_reduce(nmax[:, m:m + 1], keys[:, m, :], AX.X, ALU.max,
                                            negate=True).then_inc(nmax_ready, 1)
                for g in range(NPAIR):
                    values(g)
                    shift_q(g)
                    if g >= 1:
                        sum_q(g - 1)
                sum_q(NPAIR - 1)
                dve.wait_ge(exp_done, (n + 1) * CT)
                wait_count(dve, mt_ready, n)
                nc.vector.reciprocal(rk[:], ksum[:]).then_inc(rk_ready, 1)
                dve.wait_ge(ctx_step, (n + 1) * NPAIR)
                nc.vector.tensor_tensor(ctxm[:], kx[:, 0, 0:CT * P].rearrange("p (h k) -> p h k", h=CT),
                                        mask32[:].rearrange("p (o k) -> p o k", o=1).to_broadcast([P, CT, P]),
                                        ALU.mult).then_inc(ctx_masked, 1)
                low_q(0)
                dve.wait_ge(mthi_ready, n + 1)
                nc.vector.tensor_tensor(mtlo[:], mt[:], mthi[:].bitcast(F32), ALU.subtract).then_inc(mtlo_ready, 1)
                for g in range(NPAIR):
                    if g + 1 < NPAIR:
                        low_q(g + 1)
                    if nxt and g < PIECES:
                        low(n + 1, 1 - par, g)
                    add_x(g)

            for par in range(2):
                image(par, par, True)
            with dve.Fori(1, NIMG // 2 - 1) as it:
                for par in range(2):
                    image(2 * it + par, par, True)
            for par in range(2):
                image(NIMG - 2 + par, par, par == 0)


def phase_l1(nc, dram, sem, bnst):
    with ExitStack() as ctx:
        def sb(name, shape, dtype=F32):
            return ctx.enter_context(nc.sbuf_tensor(name, shape, dtype))

        def ps(name, shape):
            return ctx.enter_context(nc.psum_tensor(name, shape, F32))

        x1 = sb("x1", [P, CT, HW])
        wqkv = sb("wqkv", [P, CT, NU, P])
        wproj = sb("wproj", [P, 4, C])
        pwbd = sb("pwbd", [P, NU, P])
        dws = sb("dws", [P, NU, SCALE5 * SCALE5])
        pw4 = sb("pw4", [P, NU * 4, 32])
        dw4 = sb("dw4", [P, NU * 4, DY_PE])
        w4 = sb("w4", [P, NU * 4, DY_PE, 32])
        ident = sb("ident1", [P, P])
        mask8 = sb("mask8", [P, P])
        headsel = sb("headsel", [P, 2, 32])
        spread = sb("spread", [P, 2, 4, P], F32R)
        qpad = sb("qpad", [P, 2, HP * WP + NSH])
        rep = sb("rep", [P, 2, 4, RROWS * WP])
        acc = sb("acc", [P, 2, HW])
        kva = sb("kva", [P, 2, HW])
        q = sb("q", [P, 4, HW])
        kvT = sb("kvT", [P, 2, 2, 2, P + 1])
        vkraw = sb("vkraw", [P, 2, P + 1])
        vkm = sb("vkm", [P, 2, P])
        vkmT = sb("vkmT", [P, 2, P])
        dsel = sb("dsel", [P, 4, 2, 32])
        mt = sb("mt1", [P, 4, C])
        rhi = sb("rhi", [P, 2, CHUNK], F32R)
        rlo = sb("rlo", [P, 2, CHUNK], F32R)
        rcp = acc[:, 1]

        pj = ps("pj", [P, 2, 512])
        cv = ps("cv", [P, 2, 512])
        tr = ps("tr", [P, 2, 512])
        vk = ps("vk", [P, 512])
        ao = ps("ao", [P, 512])

        (w_in, x_in, zeroed, ones_set, w4_ready, pj_filled, pj_freed, rep_in0, rep_in1, tap_done,
         cv_filled, cv_freed, tr_filled, tr_freed, vk_step, vk_freed,
         vkm_ready, dsel_ready, sa_filled, sa_freed, sb_filled, sb_freed, den_filled, den_freed, r_ready,
         bc_filled, bc_freed, q_copied, rhi_ready, rlo_ready, spread_ready, y_filled, y_freed, bn_done, y_out) = (
            sem(f"l1_{n}") for n in (
                "w_in x_in zeroed ones_set w4_ready pj_filled pj_freed rep_in0 rep_in1 tap_done "
                "cv_filled cv_freed tr_filled tr_freed vk_step vk_freed "
                "vkm_ready dsel_ready sa_filled sa_freed sb_filled sb_freed den_filled den_freed r_ready "
                "bc_filled bc_freed q_copied rhi_ready rlo_ready spread_ready y_filled y_freed bn_done y_out").split())
        rep_in = (rep_in0, rep_in1)
        NW = 10
        NDEN = NCH // 2
        Y_CHUNKS = {0: (0, 1), 2: (2, 3), 3: (4, 5)}

        def padded(b):
            return qpad[:, b, 0:HP * WP].rearrange("p (r c) -> p r c", r=HP)

        def bc_bank(j):
            return (pj if j < 2 else cv)[:, j % 2]

        def y_bank(k):
            return (tr if k % 4 < 2 else cv)[:, k % 2]

        def shares(groups):
            return [range(groups * c // NCH, groups * (c + 1) // NCH) for c in range(NCH)]

        def unit_at(i, u):
            return (i, u) if u < NU else (i + 1, u - NU)

        block = ctx.enter_context(nc.Block())

        @block.sync
        def _(sp):
            sp.dma_start(x1[:], dram["x1"][0]).then_inc(x_in, 16)
            for dst, name in ((wqkv, "wqkv"), (wproj, "wproj"), (pwbd, "pwbd"), (dws, "dws"), (pw4, "pw4"),
                              (dw4, "dw4"), (ident, "ident"), (mask8, "mask8"), (headsel, "headsel"),
                              (acc[:, 0, 0:8 * P].rearrange("p (c j h) -> p c j h", c=2, j=4), "spread")):
                sp.dma_start(dst if name == "spread" else dst[:], dram[name]).then_inc(w_in, 16)

            def image(i, nxt):
                for u in range(NU):
                    v_proj = settle(sp, i * (NU * NCH) + (u + 1) * NCH)
                    v_half = [settle(sp, (NU * i + u - 1) * NCH + 3 * (h + 1))
                              for h in range(2)]
                    if u - 2 in Y_CHUNKS and not (isinstance(i, int) and i == 0):
                        chunks = Y_CHUNKS[u - 2]
                        v_y = settle(sp, 2 * NCH * (i - 1) + 2 * (chunks[-1] + 1))
                        at = settle(sp, i - 1)
                        sp.wait_ge(y_freed, v_y)
                        store_y(at, chunks)
                    if u == NU - 1 and nxt:
                        v_x = settle(sp, i * (NU * NCH) + NU * NCH)
                        at = settle(sp, i + 1)
                        sp.wait_ge(pj_filled, v_x)
                        sp.dma_start(x1[:], image_of(dram["x1"], at)).then_inc(x_in, 16)
                    sp.wait_ge(pj_freed, v_proj)
                    for h in range(2):
                        wait_count(sp, cv_filled, v_half[h])
                        for b in range(4):
                            for s in range(NSH):
                                first = h * HALF * WP + s
                                sp.dma_start(rep[32 * s:32 * s + 32, h, b, :],
                                             qpad[32 * b:32 * b + 32, u % 2, first:first + RROWS * WP]
                                             ).then_inc(rep_in[h], 16)

            def store_y(at, chunks):
                span = slice(chunks[0] * CHUNK, (chunks[-1] + 1) * CHUNK)
                sp.dma_start(image_of(dram["y"], at)[:, :, span], q[:, 2:4, span]).then_inc(y_out, 16)

            image(0, True)
            with sp.Fori(1, NIMG - 1) as i:
                image(i, True)
            image(NIMG - 1, False)
            sp.wait_ge(y_freed, 2 * NCH * NIMG)
            store_y(NIMG - 1, range(NCH))
            sp.wait_ge(y_out, 16 * (len(Y_CHUNKS) * (NIMG - 1) + 1))

        @block.tensor
        def _(pe):
            pe.wait_ge(w_in, 16 * NW)
            pe.wait_ge(w4_ready, 1)
            pe.wait_ge(spread_ready, 1)

            def project(i, u, chunks=range(NCH)):
                if u == 0:
                    pe.wait_ge(x_in, 16 * i + 16)
                for c in chunks:
                    g = i * (NU * NCH) + u * NCH + c
                    wait_count(pe, pj_freed, g - 1)
                    if u == 2 and c == 0:
                        wait_count(pe, bc_freed, 4 * NCH * i)
                    for kc in range(CT):
                        mm = nc.tensor.matmul(pj[:, c % 2, :CHUNK], wqkv[:, kc, u, :],
                                              x1[:, kc, c * CHUNK:(c + 1) * CHUNK],
                                              start=(kc == 0), stop=(kc == CT - 1))
                    mm.then_inc(pj_filled, 1)

            def convolve(i, u, chunks=range(NCH)):
                for c in chunks:
                    half, row = c // (NCH // 2), 8 * (c % (NCH // 2))
                    if c % (NCH // 2) == 0:
                        pe.wait_ge(rep_in[half], (i * NU + u + 1) * (16 * 16))
                    wait_count(pe, cv_freed, i * (NU * NCH) + u * NCH + c - 1)
                    if u == 0 and c == 0:
                        wait_count(pe, bc_freed, 4 * NCH * i)
                    if 1 <= u <= 3 and c == 0:
                        wait_count(pe, y_freed, 2 * NCH * i - (4 if u == 3 else 8))
                    if u == 4 and c == 0:
                        wait_count(pe, y_freed, 2 * NCH * i)
                    if c == 0:
                        pe.wait_ge(tap_done, (i * NU + u + 1) * NT)
                    for b in range(4):
                        taps = rep[:, half, b, :].rearrange("p (r c) -> p r c", c=WP)
                        for dy in range(DY_PE):
                            nc.tensor.matmul(cv[32 * b:32 * b + 32, c % 2, :CHUNK], w4[:, 4 * u + b, dy, :],
                                             taps[:, row + dy:row + dy + 8, 0:W],
                                             start=(dy == 0), stop=False, skip_group_check=True)
                    mm = nc.tensor.matmul(cv[:, c % 2, :CHUNK], pwbd[:, u, :], acc[:, u % 2, c * CHUNK:(c + 1) * CHUNK],
                                          start=False, stop=True, skip_group_check=True)
                    mm.then_inc(cv_filled, 1)

            def product(i, p, groups):
                u, source, half = PRODUCTS[p]
                last = (DG if source == 0 else AG) - 1
                base = i * NTR + SEG[p]

                def step(g):
                    pe.wait_ge(tr_freed, base + g + 1)
                    if g == 0:
                        wait_count(pe, vk_freed, i * 4 + p)
                        pe.wait_ge(ones_set, 1)
                    for t in range(2):
                        mm = nc.tensor.matmul(vk[:, 0:P + 1], kvT[:, g % 2, 0, t, 0:P], kvT[:, g % 2, 1, t, :],
                                              start=(g == 0 and t == 0), stop=(g == last and t == 1))
                    mm.then_inc(vk_step, 1)

                for g in groups:
                    if g == 0 and source == 0:
                        pe.wait_ge(pj_freed, i * (NU * NCH) + (u + 2) * NCH)
                    if g == 0 and source == 1:
                        pe.wait_ge(cv_freed, i * (NU * NCH) + (u + 2) * NCH)
                    wait_count(pe, tr_freed, base + (g - 1 if g >= 2 else 0))
                    if g == 0 and p:
                        wait_count(pe, y_freed, 2 * NCH * i - (8 if p < 3 else 0))
                    for t in range(2):
                        for kv in range(2):
                            if source == 0:
                                first = DFIRST + (2 * g + t) * P
                                src = qpad[:, kv, first:first + P]
                            else:
                                src = kva[:, kv, (2 * g + t) * P:(2 * g + t + 1) * P]
                            mm = nc.tensor.transpose(tr[:, g % 2, (2 * kv + t) * P:(2 * kv + t + 1) * P], src, ident[:])
                    mm.then_inc(tr_filled, 1)
                    if g >= 1:
                        step(g - 1)
                    if g == last:
                        step(g)

            def turn_product(i, p):
                pe.wait_ge(vkm_ready, 4 * i + p + 1)
                if p == 1:
                    pe.wait_ge(sa_freed, 4 * i + p)
                else:
                    wait_count(pe, sb_freed, 4 * i + p)
                nc.tensor.transpose(ao[:, 0:P], vkm[:, p % 2, :], ident[:]).then_inc(sa_filled, 1)

            def project_product(i, p):
                pe.wait_ge(sa_freed, 4 * i + max(p + 1, 2))
                wait_count(pe, sb_freed, 4 * i + p)
                nc.tensor.matmul(ao[:, P:P + C], vkmT[:, p % 2, :], wproj[:, slot_of(p), :],
                                 start=True, stop=True, skip_group_check=True).then_inc(sb_filled, 1)

            def denominators(i, d):
                if d == 0:
                    pe.wait_ge(sb_freed, 4 * i + 4)
                    pe.wait_ge(dsel_ready, 4 * i + 4)
                    pe.wait_ge(cv_freed, (i + 1) * NU * NCH)
                    pe.wait_ge(q_copied, 2 * (i + 1))
                else:
                    pe.wait_ge(den_freed, i * NDEN + d)
                for j in range(4):
                    for e in range(2):
                        c = 2 * d + e
                        mm = nc.tensor.matmul(ao[32 * j:32 * j + 32, 0:CHUNK], dsel[:, j, e, :],
                                              q[:, j, c * CHUNK:(c + 1) * CHUNK], start=(e == 0), stop=(e == 1),
                                              skip_group_check=True)
                mm.then_inc(den_filled, 1)

            def attend(i, between):
                def group(*gs):
                    if between:
                        product(i + 1, 0, gs)

                denominators(i, 0)
                group(0, 1)
                denominators(i, 1)
                group(2, 3)
                for c in range(NCH):
                    d = c // 2
                    if c % 2 == 0:
                        pe.wait_ge(rhi_ready, i * NDEN + d + 1)
                        pe.wait_ge(rlo_ready, i * NDEN + d + 1)
                    for j in range(4):
                        if c >= 1:
                            pe.wait_ge(bc_freed, 4 * NCH * i + 4 * c + j - 3)
                        elif j == 0 and between:
                            pe.wait_ge(pj_freed, (i + 1) * (NU * NCH) + 2 * NCH)
                        nc.tensor.matmul(bc_bank(j)[:, :CHUNK], spread[:, c % 2, j, :], rhi[:, d % 2, :],
                                         start=True, stop=False)
                        nc.tensor.matmul(bc_bank(j)[:, :CHUNK], spread[:, c % 2, j, :], rlo[:, d % 2, :],
                                         start=False, stop=True).then_inc(bc_filled, 1)
                    if c == 0:
                        denominators(i, 2)
                    group(c + 4)

            def output(i, chunks, u):
                pe.wait_ge(bc_freed, 4 * NCH * (i + 1))
                if u is not None:
                    pe.wait_ge(tr_freed, (i + 1) * NTR + (DG if u == 0 else SEG[3]))
                    pe.wait_ge(cv_freed, (i + 1) * (NU * NCH) + (u + 1) * NCH)
                for c in chunks:
                    for m in range(CT):
                        k = 2 * c + m
                        if c >= chunks[0] + 2:
                            pe.wait_ge(y_freed, 2 * NCH * i + k - 3)
                        for j in range(4):
                            mm = nc.tensor.matmul(y_bank(k)[:, :CHUNK], mt[:, j, m * P:(m + 1) * P],
                                                  q[:, j, c * CHUNK:(c + 1) * CHUNK], start=(j == 0), stop=(j == 3))
                        mm.then_inc(y_filled, 1)

            def image(i, prev, nxt):
                for u in range(NU):
                    if u == 0 and prev:
                        attend(i - 1, True)
                    elif u == 0:
                        product(i, 0, range(DG))
                    if u in (4, 5):
                        turn_product(i, u - 2)
                    for c, groups in enumerate(shares(DG)):
                        convolve(i, u, [c])
                        if u == 2:
                            product(i, 2, groups)
                    for c, groups in enumerate(shares(AG)):
                        if u + 2 < NU or nxt:
                            project(*unit_at(i, u + 2), [c])
                        if u in (1, 4):
                            product(i, 1 if u == 1 else 3, groups)
                    if u in Y_CHUNKS and prev:
                        output(i - 1, Y_CHUNKS[u], u)
                    if u == 1:
                        turn_product(i, 0)
                    if u == 2:
                        turn_product(i, 1)
                    if u == 3:
                        project_product(i, 0)
                        project_product(i, 1)
                    if u == 4:
                        project_product(i, 2)
                    if u == 5:
                        project_product(i, 3)

            project(0, 0)
            project(0, 1)
            image(0, False, True)
            with pe.Fori(1, NIMG - 1) as i:
                image(i, True, True)
            image(NIMG - 1, True, False)
            attend(NIMG - 1, False)
            output(NIMG - 1, range(NCH), None)

        @block.scalar
        def _(act):
            act.wait_ge(w_in, 16 * NW)
            nc.scalar.copy(spread[:], acc[:, 0, 0:8 * P].rearrange("p (c j h) -> p c j h", c=2, j=4)
                           ).then_inc(spread_ready, 1)
            act.wait_ge(zeroed, 1)

            def project(i, u, chunks=range(NCH)):
                if chunks[0] == 0 and not (isinstance(i, int) and i == 0 and u < 2):
                    act.wait_ge(tap_done, (i * NU + u - 1) * NT)
                    for h in range(2):
                        act.wait_ge(rep_in[h], (i * NU + u - 1) * 256)
                    if u in (0, 1):
                        act.wait_ge(tr_filled, i * NTR - AG)
                    if u in (2, 3):
                        act.wait_ge(tr_filled, i * NTR + DG)
                    if u in (4, 5):
                        act.wait_ge(tr_filled, i * NTR + SEG[3])
                    if u == 0 or u == 1:
                        wait_count(act, q_copied, 2 * (i - 1) + u + 1)
                for c in chunks:
                    act.wait_ge(pj_filled, i * (NU * NCH) + u * NCH + c + 1)
                    src = pj[:, c % 2, :CHUNK]
                    dst = padded(u % 2)[:, PAD + 8 * c:PAD + 8 * c + 8, PAD:PAD + W]
                    nc.scalar.copy(dst, src.rearrange("p (r c) -> p r c", c=W)).then_inc(pj_freed, 1)

            def copy_queries(i, u):
                act.wait_ge(pj_freed, i * (NU * NCH) + (u + 1) * NCH)
                wait_count(act, y_filled, 2 * NCH * i)
                nc.scalar.activation(q[:, HALVES[u]].rearrange("p (r c) -> p r c", c=W),
                                     padded(u % 2)[:, PAD:PAD + H, PAD:PAD + W], ACT.Relu).then_inc(q_copied, 1)

            def convolve(i, u, chunks=range(NCH)):
                if chunks[0] == 0:
                    if u < 4:
                        wait_count(act, tr_filled, i * NTR + (SEG[2] if u >= 2 else 0))
                    else:
                        wait_count(act, y_out, 16 * len(Y_CHUNKS) * i)
                for c in chunks:
                    if u == 4:
                        wait_count(act, bn_done, 2 * NCH * (i - 1) + 2 * c + 2)
                    act.wait_ge(cv_filled, i * (NU * NCH) + u * NCH + c + 1)
                    span = slice(c * CHUNK, (c + 1) * CHUNK)
                    if PARTS[u] == 0:
                        dst = q[:, 2 + HALVES[u], span]
                    else:
                        dst = kva[:, PARTS[u] - 1, span]
                    nc.scalar.activation(dst, cv[:, c % 2, :CHUNK], ACT.Copy if PARTS[u] == 2 else ACT.Relu
                                         ).then_inc(cv_freed, 1)

            def product(i, p, groups):
                _, source, _ = PRODUCTS[p]
                last = (DG if source == 0 else AG) - 1
                base = i * NTR + SEG[p]
                for g in groups:
                    act.wait_ge(tr_filled, base + g + 1)
                    wait_count(act, vk_step, base + (g - 1 if g >= 2 else 0))
                    bank = tr[:, g % 2, :].rearrange("p (x t c) -> p x t c", x=2, t=2)
                    if source == 0:
                        nc.scalar.activation(kvT[:, g % 2, 0, :, 0:P], bank[:, 0], ACT.Relu)
                        nc.scalar.copy(kvT[:, g % 2, 1, :, 0:P], bank[:, 1]).then_inc(tr_freed, 1)
                    else:
                        nc.scalar.copy(kvT[:, g % 2, :, :, 0:P], bank).then_inc(tr_freed, 1)
                    if g == last:
                        act.wait_ge(vk_step, base + last + 1)
                        wait_count(act, dsel_ready, 4 * i + p - 1)
                        nc.scalar.copy(vkraw[:, p % 2, :], vk[:, 0:P + 1]).then_inc(vk_freed, 1)

            def attend(i, between):
                groups = ((0, 1), (2, 3), (4, 5, 6))
                for d in range(NDEN):
                    if between:
                        product(i + 1, 0, groups[d])
                    act.wait_ge(r_ready, i * NDEN + d + 1)
                    wait_count(act, bc_filled, 4 * NCH * i + (8 if d == 2 else 0))
                    nc.scalar.copy(rhi[:, d % 2, :], rcp[:, d * CHUNK:(d + 1) * CHUNK]).then_inc(rhi_ready, 1)
                if between:
                    product(i + 1, 0, range(groups[-1][-1] + 1, DG))

            def turn_product(i, p):
                act.wait_ge(sa_filled, 4 * i + p + 1)
                nc.scalar.copy(vkmT[:, p % 2, :], ao[:, 0:P]).then_inc(sa_freed, 1)

            def project_product(i, p):
                act.wait_ge(sb_filled, 4 * i + p + 1)
                if not (isinstance(i, int) and i == 0):
                    act.wait_ge(y_filled, 2 * NCH * i)
                nc.scalar.copy(mt[:, slot_of(p), :], ao[:, P:P + C]).then_inc(sb_freed, 1)

            def output(i, chunks):
                for c in chunks:
                    for m in range(CT):
                        act.wait_ge(y_filled, 2 * NCH * i + 2 * c + 2)
                        nc.scalar.copy(q[:, 2 + m, c * CHUNK:(c + 1) * CHUNK], y_bank(2 * c + m)[:, :CHUNK]
                                       ).then_inc(y_freed, 1)

            def image(i, prev, nxt):
                for u in range(NU):
                    if u == 0 and prev:
                        attend(i - 1, True)
                    elif u == 0:
                        product(i, 0, range(DG))
                    if u in (4, 5):
                        turn_product(i, u - 2)
                    for c, groups in enumerate(shares(DG)):
                        convolve(i, u, [c])
                        if u == 2:
                            product(i, 2, groups)
                    for c, groups in enumerate(shares(AG)):
                        if u + 2 < NU or nxt:
                            project(*unit_at(i, u + 2), [c])
                        if u in (1, 4):
                            product(i, 1 if u == 1 else 3, groups)
                    if u in Y_CHUNKS and prev:
                        output(i - 1, Y_CHUNKS[u])
                    if u == 1:
                        turn_product(i, 0)
                    if u == 2:
                        turn_product(i, 1)
                    if u == 3:
                        project_product(i, 0)
                        project_product(i, 1)
                        copy_queries(i, 4)
                    if u == 4:
                        copy_queries(i, 5)
                        project_product(i, 2)
                    if u == 5:
                        project_product(i, 3)

            project(0, 0)
            project(0, 1)
            image(0, False, True)
            with act.Fori(1, NIMG - 1) as i:
                image(i, True, True)
            image(NIMG - 1, True, False)
            attend(NIMG - 1, False)
            output(NIMG - 1, range(NCH))

        @block.gpsimd
        def _(pool):
            nc.gpsimd.memset(qpad[:], 0.0).then_inc(zeroed, 1)
            nc.gpsimd.memset(kvT[:, :, 1, :, P:P + 1], 1.0).then_inc(ones_set, 1)
            pool.wait_ge(w_in, 16 * NW)

            def image(i):
                for p in range(4):
                    pool.wait_ge(vk_freed, 4 * i + p + 1)
                    if p >= 2:
                        pool.wait_ge(sa_filled, 4 * i + p - 1)
                    else:
                        wait_count(pool, sa_filled, 4 * i)
                    nc.gpsimd.tensor_tensor(vkm[:, p % 2, :], vkraw[:, p % 2, 0:P], mask8[:], ALU.mult).then_inc(vkm_ready, 1)
                    wait_count(pool, den_filled, NDEN * i)
                    nc.gpsimd.tensor_tensor(dsel[:, slot_of(p)].rearrange("p e h -> p (e h)"),
                                            headsel[:].rearrange("p e h -> p (e h)"),
                                            vkraw[:, p % 2, P:P + 1].to_broadcast([P, 64]), ALU.mult
                                            ).then_inc(dsel_ready, 1)

            def attend(i):
                for d in range(NDEN):
                    pool.wait_ge(rhi_ready, i * NDEN + d + 1)
                    wait_count(pool, bc_filled, 4 * NCH * i + (8 if d == 2 else 0))
                    nc.gpsimd.tensor_tensor(rlo[:, d % 2, :], rcp[:, d * CHUNK:(d + 1) * CHUNK],
                                            rhi[:, d % 2, :].bitcast(F32), ALU.subtract).then_inc(rlo_ready, 1)

            image(0)
            with pool.Fori(1, NIMG) as i:
                attend(i - 1)
                image(i)
            attend(NIMG - 1)

        @block.vector
        def _(dve):
            dve.wait_ge(w_in, 16 * NW)
            dve.wait_ge(spread_ready, 1)
            nc.vector.tensor_tensor(w4[:], pw4[:].rearrange("p b (o c) -> p b o c", o=1).to_broadcast([P, NU * 4, DY_PE, 32]),
                                    dw4[:].rearrange("p b (r o) -> p b r o", o=1).to_broadcast([P, NU * 4, DY_PE, 32]),
                                    ALU.mult).then_inc(w4_ready, 1)

            def taps(i, u, between=None):
                dve.wait_ge(pj_freed, i * (NU * NCH) + (u + 1) * NCH)
                wait_count(dve, cv_filled, (i * NU + u - 1) * NCH)
                a = acc[:, u % 2].rearrange("p (r c) -> p r c", c=W)
                for k, (dy, dx) in enumerate(DVE_TAPS):
                    if between and k == NT // 3:
                        between()
                    src = padded(u % 2)[:, dy:dy + H, dx:dx + W]
                    w = dws[:, u, SCALE5 * dy + dx:SCALE5 * dy + dx + 1]
                    if k == 0:
                        op = nc.vector.tensor_scalar(a, src, w, None, ALU.mult)
                    else:
                        dve.wait_ge(tap_done, (i * NU + u) * NT + k)
                        op = nc.vector.scalar_tensor_tensor(out=a, in0=src, scalar=w, in1=a, op0=ALU.mult, op1=ALU.add)
                    op.then_inc(tap_done, 1)

            def reciprocals(i, d):
                dve.wait_ge(den_filled, i * NDEN + d + 1)
                r = rcp[:, d * CHUNK:(d + 1) * CHUNK]
                nc.vector.tensor_scalar(r, ao[:, 0:CHUNK], EPS_ATT, None, ALU.add).then_inc(den_freed, 1)
                dve.wait_ge(den_freed, i * NDEN + d + 1)
                nc.vector.reciprocal(r, r).then_inc(r_ready, 1)

            def attend(i):
                reciprocals(i, 0)
                for c in range(NCH):
                    if c % 2 == 0 and c // 2 + 1 < NDEN:
                        reciprocals(i, c // 2 + 1)
                    for j in range(4):
                        k = 4 * c + j
                        dve.wait_ge(bc_filled, 4 * NCH * i + k + 1)
                        qc = q[:, j, c * CHUNK:(c + 1) * CHUNK]
                        nc.vector.tensor_tensor(qc, qc, bc_bank(j)[:, :CHUNK], ALU.mult).then_inc(bc_freed, 1)

            def statistics(i, chunks):
                for c in chunks:
                    for m in range(CT):
                        dve.wait_ge(y_freed, 2 * NCH * i + 2 * c + m + 1)
                        nc.vector.bn_stats(bnst_at(i, m, c), q[:, 2 + m, c * CHUNK:(c + 1) * CHUNK]).then_inc(bn_done, 1)

            def bnst_at(i, m, c):
                if isinstance(i, int):
                    return bnst[:, m, i, c, :]
                return bnst[:, m, bass.ds(i, 1), c, :].rearrange("p o s -> p (o s)")

            def image(i, prev):
                taps(i, 0)
                if prev:
                    attend(i - 1)
                for u in range(1, NU):
                    if prev and u - 2 in Y_CHUNKS:
                        taps(i, u, lambda: statistics(i - 1, Y_CHUNKS[u - 2]))
                    else:
                        taps(i, u)

            image(0, False)
            with dve.Fori(1, NIMG) as i:
                image(i, True)
            attend(NIMG - 1)
            statistics(NIMG - 1, range(NCH))


def phase_out(nc, dram, sem, bnst):
    with ExitStack() as ctx:
        def sb(name, shape):
            return ctx.enter_context(nc.sbuf_tensor(name, shape, F32))

        RING = 4
        yb = sb("yb", [P, RING, CT, HW])
        xb = sb("xb", [P, RING, CT, HW])
        gb = sb("gb", [P, 2, CT])
        agg = sb("agg", [P, CT, 2])
        ve = sb("ve", [P, CT])
        rt = sb("rt", [P, CT])
        r0 = sb("r0", [P, CT])
        t0 = sb("t0", [P, CT])
        sc = sb("sc", [P, CT])
        sh = sb("sh", [P, CT])

        g_in, stat, root, load0, load1, load2, load3, scaled, summed, store0, store1, store2, store3 = (
            sem(f"out_{n}") for n in
            "g_in stat root load0 load1 load2 load3 scaled summed store0 store1 store2 store3".split())
        load, store = (load0, load1, load2, load3), (store0, store1, store2, store3)

        block = ctx.enter_context(nc.Block())

        @block.sync
        def _(sp):
            sp.dma_start(gb[:], dram["gb"]).then_inc(g_in, 16)
            for n in range(NIMG):
                r = n % RING
                if n >= RING:
                    sp.wait_ge(store[r], 16 * (n // RING))
                sp.dma_start(yb[:, r], dram["y"][n]).then_inc(load[r], 16)
                sp.dma_start(xb[:, r], dram["x1"][n]).then_inc(load[r], 16)

        @block.gpsimd
        def _(pool):
            for n in range(NIMG):
                r = n % RING
                pool.wait_ge(summed, n + 1)
                pool.dma_start(dram["out"][n], yb[:, r]).then_inc(store[r], 16)
            for r in range(RING):
                pool.wait_ge(store[r], 16 * (NIMG // RING))

        @block.scalar
        def _(act):
            act.wait_ge(stat, CT + 1)
            nc.scalar.activation(rt[:], ve[:], ACT.Sqrt).then_inc(root, 1)
            act.wait_ge(stat, CT + 9)
            for n in range(NIMG):
                r = n % RING
                act.wait_ge(load[r], 32 * (n // RING + 1))
                for m in range(CT):
                    last = nc.scalar.activation(yb[:, r, m], yb[:, r, m], ACT.Identity, bias=sh[:, m:m + 1], scale=sc[:, m:m + 1])
                last.then_inc(scaled, 1)

        @block.vector
        def _(dve):
            done = [0]

            def step(op):
                done[0] += 1
                op.then_inc(stat, 1)
                dve.wait_ge(stat, done[0])

            for m in range(CT):
                step(nc.vector.bn_aggr(agg[:, m], bnst[:, m].rearrange("p i c s -> p (i c s)")))
            step(nc.vector.tensor_scalar(ve[:], agg[:, :, 1], EPS_BN, None, ALU.add))
            dve.wait_ge(root, 1)
            dve.wait_ge(g_in, 16)
            step(nc.vector.reciprocal(r0[:], rt[:]))
            step(nc.vector.tensor_tensor(t0[:], r0[:], r0[:], ALU.mult))
            step(nc.vector.tensor_tensor(t0[:], t0[:], ve[:], ALU.mult))
            step(nc.vector.tensor_scalar(t0[:], t0[:], -0.5, 1.5, ALU.mult, ALU.add))
            step(nc.vector.tensor_tensor(r0[:], r0[:], t0[:], ALU.mult))
            step(nc.vector.tensor_tensor(sc[:], r0[:], gb[:, 0], ALU.mult))
            step(nc.vector.tensor_tensor(t0[:], agg[:, :, 0], sc[:], ALU.mult))
            nc.vector.tensor_tensor(sh[:], gb[:, 1], t0[:], ALU.subtract).then_inc(stat, 1)
            for n in range(NIMG):
                r = n % RING
                dve.wait_ge(scaled, n + 1)
                nc.vector.tensor_tensor(yb[:, r], yb[:, r], xb[:, r], ALU.add).then_inc(summed, 1)


def build(nc, dram):
    with ExitStack() as ctx:
        def sem(name):
            return ctx.enter_context(nc.semaphore(name))

        bnst = ctx.enter_context(nc.sbuf_tensor("bnst", [P, CT, NIMG, NCH, 6], F32))
        phase_l0(nc, dram, sem)
        phase_l1(nc, dram, sem, bnst)
        phase_out(nc, dram, sem, bnst)


def layouts(inputs):
    import numpy as np

    a = {n: np.ascontiguousarray(v) for n, v in inputs.items()}

    def columns(v, parts):
        return v.reshape(parts, P).T

    out = {}
    out["x"] = a["x"].reshape(NIMG, CT, P, HW).transpose(0, 2, 1, 3)
    wkqv = np.concatenate([a["L0_conv_Wk"].T, a["L0_conv_Wq"].T, a["L0_conv_Wv"].T], 1)
    out["wkqv"] = wkqv.reshape(CT, P, 3 * C).transpose(1, 0, 2)
    out["wp"] = a["L0_conv_Wp"].T.reshape(CT, P, C).transpose(1, 0, 2)
    out["bqv"] = np.broadcast_to(np.stack([a["L0_conv_bq"], a["L0_conv_bv"]]), (P, 2, C))
    out["bkp"] = np.stack([columns(a["L0_conv_bk"], CT), columns(a["L0_conv_bp"], CT)], 1)

    rows = np.array([[3 * DIM * h + DIM * PARTS[u] + d for h in range(16 * HALVES[u], 16 * HALVES[u] + 16)
                      for d in range(DIM)] for u in range(NU)])
    wq = a["L1_conv_w_qkv"][rows]
    out["wqkv"] = wq.transpose(2, 0, 1).reshape(CT, P, NU, P).transpose(1, 0, 2, 3)
    out["wproj"] = a["L1_conv_w_proj"].T.reshape(4, P, C).transpose(1, 0, 2)
    pw = a["L1_conv_w_pw"][rows[:, ::DIM] // DIM]
    bd = np.zeros((NU, P, P), pw.dtype)
    for g in range(16):
        bd[:, 8 * g:8 * g + 8, 8 * g:8 * g + 8] = pw[:, g].transpose(0, 2, 1)
    out["pwbd"] = bd.transpose(1, 0, 2)
    blocks = np.stack([bd[:, 32 * b:32 * b + 32, 32 * b:32 * b + 32] for b in range(4)], 1)
    out["pw4"] = np.tile(blocks.reshape(NU * 4, 32, 32).transpose(1, 0, 2), (NSH, 1, 1))
    dw = a["L1_conv_w_dw"].reshape(-1, SCALE5, SCALE5)[rows]
    out["dws"] = dw.reshape(NU, P, SCALE5 * SCALE5).transpose(1, 0, 2)
    stack = dw[:, :, :DY_PE, :NSH].reshape(NU, 4, 32, DY_PE, NSH)
    out["dw4"] = stack.transpose(4, 2, 0, 1, 3).reshape(P, NU * 4, DY_PE)
    out["gb"] = np.stack([columns(a["L1_conv_bn_gamma"], CT), columns(a["L1_conv_bn_beta"], CT)], 1)

    k = np.arange(P)
    out["ident"] = np.eye(P, dtype=np.float32)
    out["mask32"] = (k[:, None] // HD0 == k[None] // HD0).astype(np.float32)
    out["mask8"] = (k[:, None] // DIM == k[None] // DIM).astype(np.float32)
    head = 16 * np.arange(2)[None, :, None] + k[:, None, None] // DIM
    out["headsel"] = (head == np.arange(32)[None, None]).astype(np.float32)
    j = np.arange(4)
    row, half = k[:, None, None, None], 16 * np.arange(2)[None, :, None, None]
    out["spread"] = ((row // 32 == j[None, None, :, None]) & (row % 32 == half + k[None, None, None] // DIM)
                     ).astype(np.float32)
    return {n: np.ascontiguousarray(v) for n, v in out.items()}


def kernel(**inputs):
    import numpy as _np
    import concourse.bacc as _bacc
    from concourse.bass_utils import run_bass_kernel_spmd as _run

    nc = _bacc.Bacc("TRN2", target_bir_lowering=False, num_devices=1)
    arrays, dram = {}, {}
    for name, a in layouts(inputs).items():
        arrays[f"in_{name}"] = a
        dram[name] = nc.dram_tensor(f"in_{name}", a.shape, mybir.dt.from_np(a.dtype), kind="ExternalInput").ap()
    for name in ("x1", "y"):
        dram[name] = nc.dram_tensor(f"scratch_{name}", (NIMG, P, CT, HW), F32).ap()
    dram["out"] = nc.dram_tensor("out_0", (NIMG, P, CT, HW), F32, kind="ExternalOutput").ap()
    build(nc, dram)
    r = _run(nc, [arrays], core_ids=[0])
    got = r.results[0]["out_0"]
    return _np.ascontiguousarray(got.transpose(0, 2, 1, 3)).reshape(NIMG, C, H, W)
```

```python
from contextlib import ExitStack

import concourse.bass as bass
from concourse import mybir
from concourse.alu_op_type import AluOpType as ALU

ACT = mybir.ActivationFunctionType
F32 = mybir.dt.float32
F32R = mybir.dt.float32r
AX = mybir.AxisListType

P = 128
NIMG, C, H, W = 8, 256, 48, 48
HW = H * W
CT = C // P
CHUNK = 8 * W
NCH = HW // CHUNK

HEADS0, HD0 = 8, 32
PAIR = 2 * P
NPAIR = HW // PAIR

DIM, SCALE5, PAD = 8, 5, 2
HP, WP = H + 2 * PAD, W + 2 * PAD
NU = 6
PARTS = (1, 2, 1, 2, 0, 0)
HALVES = (0, 0, 1, 1, 0, 1)
EPS_ATT, EPS_BN = 1e-15, 1e-5
DY_PE = 3
NSH = 4
HALF = H // 2
RROWS = HALF + DY_PE - 1
DVE_TAPS = [(dy, dx) for dy in range(SCALE5) for dx in range(SCALE5) if not (dy < DY_PE and dx < NSH)]
NT = len(DVE_TAPS)
DG, AG = 10, HW // (2 * P)
DFIRST = PAD * WP - (DG * 2 * P - H * WP) // 2
assert DFIRST >= 0 and DFIRST + DG * 2 * P <= HP * WP and DFIRST + DG * 2 * P >= (PAD + H) * WP
PRODUCTS = ((0, 0, 0), (0, 1, 0), (2, 0, 1), (2, 1, 1))
SEG = (0, DG, DG + AG, 2 * DG + AG)
NTR = 2 * (DG + AG)


def slot_of(product):
    _, source, half = PRODUCTS[product]
    return 2 * source + half


def wait_count(eng, sem, value):
    if isinstance(value, int) and value <= 0:
        return
    eng.wait_ge(sem, value)


def settle(eng, value):
    return value if isinstance(value, int) else eng.snap(value)


def image_of(array, i):
    return array[i] if isinstance(i, int) else array[bass.ds(i, 1)].rearrange("o p c t -> p (o c) t")


def cut(array, *shapes):
    pieces, first = [], 0
    for shape in shapes:
        size = 1
        for n in shape:
            size *= n
        names = "abc"[:len(shape)]
        pieces.append(array[:, first:first + size].rearrange(
            f"p ({' '.join(names)}) -> p {' '.join(names)}", **{k: n for k, n in zip(names, shape)}))
        first += size
    return pieces


def phase_l0(nc, dram, sem):
    with ExitStack() as ctx:
        def sb(name, shape, dtype=F32):
            return ctx.enter_context(nc.sbuf_tensor(name, shape, dtype))

        def ps(name, shape):
            return ctx.enter_context(nc.psum_tensor(name, shape, F32))

        xs = sb("xs", [P, 2, CT, HW])
        xhi = sb("xhi", [P, 2, CT, HW], F32R)
        xlo = sb("xlo", [P, 2, CT, HW], F32R)
        wkqv = sb("wkqv", [P, CT, 3 * C])
        whi = sb("whi", [P, CT, 3 * C], F32R)
        wlo = sb("wlo", [P, CT, 3 * C], F32R)
        wp = sb("wp", [P, CT, C])
        bqv = sb("bqv", [P, 2, C])
        bkp = sb("bkp", [P, 2, CT])
        ident = sb("ident0", [P, P])
        mask32 = sb("mask32", [P, P])
        keys = sb("keys", [P, CT, HW])
        nmax = sb("nmax", [P, CT])
        ksum = sb("ksum", [P, CT])
        rk = sb("rk", [P, CT])
        vT = sb("vT", [P, HW // P, C])
        ekT = sb("ekT", [P, 2, 2, C])
        ctxm = sb("ctxm", [P, CT, P])
        qs = sb("qs", [P, NPAIR, 2, HEADS0, HD0])
        qmx = sb("qmx", [P, 2, 2 * HEADS0])
        qsm = sb("qsm", [P, 2, 2 * HEADS0])
        qrc = sb("qrc", [P, 2, 2 * HEADS0])
        mthi = sb("mthi", [P, CT, C], F32R)
        mtlo = sb("mtlo", [P, CT, C], F32R)
        qnhi = sb("qnhi", [P, 2, CT, PAIR], F32R)
        qnlo = sb("qnlo", [P, 2, CT, PAIR], F32R)

        kx = ps("kx", [P, 2, 512])
        qv = ps("qv", [P, 4, 512])
        ep = ps("ep", [P, 2, 512])

        def ebank(n):
            return ep[:, n % 2, :].rearrange("p (t c) -> p t c", t=2)

        (w_in, wkqv_in, w_hi, w_lo, x_in0, x_in1, x_out0, x_out1, hi_ready, lo_ready, k_filled, k_freed, nmax_ready, exp_done,
         qv_filled, v_done, q_added, e_filled, e_freed, ctx_step, ctx_masked, rk_ready, m_filled, mthi_ready, mtlo_ready, qnlo_ready, q_maxed,
         q_shifted, q_exp, q_summed, q_recip, q_ready, x_filled, x1_done) = (
            sem(f"l0_{n}") for n in (
                "w_in wkqv_in w_hi w_lo x_in0 x_in1 x_out0 x_out1 hi_ready lo_ready k_filled k_freed nmax_ready exp_done "
                "qv_filled v_done q_added e_filled e_freed ctx_step ctx_masked rk_ready m_filled mthi_ready mtlo_ready qnlo_ready q_maxed "
                "q_shifted q_exp q_summed q_recip q_ready x_filled x1_done").split())
        x_in, x_out = (x_in0, x_in1), (x_out0, x_out1)
        NW = 5
        NE = 2 * NPAIR
        NK = CT * NCH
        PIECES = 4
        PIECE = HW // PIECES
        x_first = [sem(f"l0_x_first{s}") for s in range(PIECES)]

        def piece(array, par, s):
            return array[:, par, :, s * PIECE:(s + 1) * PIECE]

        def split_input(eng, par, it):
            eng.wait_ge(x_in[1 - par], (it + 1) * 16)
            return 1 - par

        block = ctx.enter_context(nc.Block())

        @block.sync
        def _(sp):
            sp.dma_start(wkqv[:], dram["wkqv"]).then_inc(wkqv_in, 16)
            for s in range(PIECES):
                sp.dma_start(piece(xs, 0, s), dram["x"][0][:, :, s * PIECE:(s + 1) * PIECE]).then_inc(x_first[s], 16)
            for dst, name in ((wp, "wp"), (bqv, "bqv"), (bkp, "bkp"), (ident, "ident"), (mask32, "mask32")):
                sp.dma_start(dst[:], dram[name]).then_inc(w_in, 16)
            sp.dma_start(xs[:, 1], dram["x"][1]).then_inc(x_in[1], 16)
            with sp.Fori(0, NIMG // 2 - 1) as it:
                for par in range(2):
                    written = sp.snap((2 * it + par + 1) * NPAIR)
                    stored = sp.snap((it + 1) * 16)
                    here = sp.snap(2 * it + par)
                    there = sp.snap(2 * it + par + 2)
                    sp.wait_ge(x1_done, written)
                    sp.dma_start(image_of(dram["x1"], here),
                                 xs[:, par]).then_inc(x_out[par], 16)
                    sp.wait_ge(x_out[par], stored)
                    sp.dma_start(xs[:, par], image_of(dram["x"], there)).then_inc(x_in[par], 16)
            for par in range(2):
                n = NIMG - 2 + par
                sp.wait_ge(x1_done, (n + 1) * NPAIR)
                sp.dma_start(dram["x1"][n], xs[:, par]).then_inc(x_out[par], 16)
            for par in range(2):
                sp.wait_ge(x_out[par], 16 * NIMG // 2)

        @block.tensor
        def _(pe):
            pe.wait_ge(w_in, 16 * NW)
            pe.wait_ge(w_hi, 1)
            pe.wait_ge(w_lo, 1)

            def product3(out, left, right, start, stop):
                (lhi, llo), (rhi, rlo) = left, right
                nc.tensor.matmul(out, lhi, rhi, start=start, stop=False, skip_group_check=True)
                nc.tensor.matmul(out, lhi, rlo, start=False, stop=False, skip_group_check=True)
                return nc.tensor.matmul(out, llo, rhi, start=False, stop=stop, skip_group_check=True)

            def image(n, par):
                def x_part(kc, first, size):
                    return tuple(x[:, par, kc, first:first + size] for x in (xhi, xlo))

                def w_part(kc, first, size):
                    return tuple(w[:, kc, first:first + size] for w in (whi, wlo))

                def key_group(g):
                    m, c = g // NCH, g % NCH
                    if g < 2:
                        wait_count(pe, x1_done, n * NPAIR - 1 + g)
                    else:
                        pe.wait_ge(k_freed, n * NK + g - 1)
                    for kc in range(CT):
                        mm = product3(kx[:, (g + 1) % 2, :CHUNK], w_part(kc, m * P, P), x_part(kc, c * CHUNK, CHUNK),
                                      kc == 0, kc == CT - 1)
                    mm.then_inc(k_filled, 1)

                def token_major(g):
                    wait_count(pe, v_done, n * NPAIR + g - 1)
                    wait_count(pe, q_added, n * NPAIR + g - 1)
                    for t in range(2):
                        for kc in range(CT):
                            mm = product3(qv[:, 2 * (g % 2) + t, :], x_part(kc, (2 * g + t) * P, P),
                                          w_part(kc, C, 2 * C), kc == 0, kc == CT - 1)
                    mm.then_inc(qv_filled, 1)

                def turn_keys(g):
                    if g == 0:
                        pe.wait_ge(exp_done, (n + 1) * CT)
                    wait_count(pe, e_freed, n * NE + g - 1)
                    if g < 2:
                        wait_count(pe, qnlo_ready, n * NPAIR)
                    for t in range(2):
                        for h in range(CT):
                            mm = nc.tensor.transpose(ebank(g)[:, t, h * P:(h + 1) * P],
                                                     keys[:, h, (2 * g + t) * P:(2 * g + t + 1) * P], ident[:])
                    mm.then_inc(e_filled, 1)

                def context(g):
                    pe.wait_ge(e_freed, n * NE + g + 1)
                    pe.wait_ge(v_done, n * NPAIR + g + 1)
                    if g == 0:
                        pe.wait_ge(k_freed, (n + 1) * NK)
                    for t in range(2):
                        for h in range(CT):
                            mm = nc.tensor.matmul(kx[:, 0, h * P:(h + 1) * P],
                                                  vT[:, 2 * g + t, h * P:(h + 1) * P],
                                                  ekT[:, g % 2, t, h * P:(h + 1) * P],
                                                  start=(g == 0 and t == 0 and h == 0),
                                                  stop=(g == NPAIR - 1 and t == 1), skip_group_check=True)
                    mm.then_inc(ctx_step, 1)

                def turn_queries(g):
                    k = NPAIR + g
                    pe.wait_ge(q_ready, n * NPAIR + g + 1)
                    pe.wait_ge(e_freed, n * NE + k - 1)
                    if g >= 2:
                        pe.wait_ge(qnlo_ready, n * NPAIR + g - 1)
                    for t in range(2):
                        for h in range(CT):
                            src = qs[:, g, t, 4 * h:4 * h + 4, :].rearrange("p a b -> p (a b)")
                            mm = nc.tensor.transpose(ebank(k)[:, h, t * P:(t + 1) * P], src, ident[:])
                    mm.then_inc(e_filled, 1)

                def x1_group(g):
                    pe.wait_ge(e_freed, n * NE + NPAIR + g + 1)
                    pe.wait_ge(qnlo_ready, n * NPAIR + g + 1)
                    if g == 0:
                        pe.wait_ge(mthi_ready, (n + 1) * CT)
                        pe.wait_ge(mtlo_ready, (n + 1) * CT)
                    if g >= 2:
                        pe.wait_ge(x1_done, n * NPAIR + g - 1)
                    for m in range(CT):
                        for kc in range(CT):
                            mm = product3(kx[:, g % 2, m * PAIR:(m + 1) * PAIR],
                                          tuple(a[:, kc, m * P:(m + 1) * P] for a in (mthi, mtlo)),
                                          tuple(a[:, g % 2, kc, :] for a in (qnhi, qnlo)), kc == 0, kc == CT - 1)
                    mm.then_inc(x_filled, 1)

                pe.wait_ge(hi_ready, (n + 1) * PIECES)
                pe.wait_ge(lo_ready, (n + 1) * PIECES)
                for g in range(NK):
                    key_group(g)
                for g in range(NPAIR):
                    token_major(g)
                    if g >= 2:
                        turn_keys(g - 2)
                    if g >= 3:
                        context(g - 3)
                for g in range(NPAIR - 2, NPAIR):
                    turn_keys(g)
                    context(g - 1)
                turn_queries(0)
                context(NPAIR - 1)
                turn_queries(1)
                pe.wait_ge(ctx_masked, n + 1)
                for h in range(CT):
                    mm = nc.tensor.matmul(kx[:, 1, h * C:(h + 1) * C], ctxm[:, h], wp[:, h],
                                          start=True, stop=True, skip_group_check=True)
                mm.then_inc(m_filled, 1)
                for g in range(NPAIR):
                    if 1 <= g < NPAIR - 1:
                        turn_queries(g + 1)
                    x1_group(g)

            for par in range(2):
                image(par, par)
            with pe.Fori(1, NIMG // 2) as it:
                for par in range(2):
                    image(2 * it + par, par)

        @block.scalar
        def _(act):
            act.wait_ge(wkqv_in, 16)
            nc.scalar.copy(whi[:], wkqv[:]).then_inc(w_hi, 1)

            def high(par, s):
                nc.scalar.copy(piece(xhi, par, s), piece(xs, par, s)).then_inc(hi_ready, 1)

            for s in range(PIECES):
                act.wait_ge(x_first[s], 16)
                high(0, s)
            act.wait_ge(w_in, 16 * NW)

            def image(n, par, it, nxt):
                def exponentials(g):
                    act.wait_ge(e_filled, n * NE + g + 1)
                    wait_count(act, ctx_step, n * NPAIR + g - 1)
                    nc.scalar.copy(ekT[:, g % 2], ebank(g)).then_inc(e_freed, 1)

                def exp_q(g):
                    act.wait_ge(q_shifted, n * NPAIR + g + 1)
                    nc.scalar.activation(qs[:, g], qs[:, g], ACT.Exp).then_inc(q_exp, 1)

                wait_count(act, e_filled, n * NE)
                for g in range(NK):
                    m, c = g // NCH, g % NCH
                    act.wait_ge(k_filled, n * NK + g + 1)
                    nc.scalar.activation(keys[:, m, c * CHUNK:(c + 1) * CHUNK], kx[:, (g + 1) % 2, :CHUNK],
                                         ACT.Identity, bias=bkp[:, 0, m:m + 1]).then_inc(k_freed, 1)
                wait_count(act, rk_ready, n)
                for m in range(CT):
                    act.wait_ge(nmax_ready, n * CT + m + 1)
                    nc.scalar.activation(keys[:, m, :], keys[:, m, :], ACT.Exp, bias=nmax[:, m:m + 1],
                                         accum_out=ksum[:, m:m + 1]).then_inc(exp_done, 1)
                for g in range(NPAIR):
                    if g >= 2:
                        exponentials(g - 2)
                    exp_q(g)
                    if nxt and 5 <= g < 5 + PIECES:
                        if g == 5:
                            wait_count(act, qv_filled, n * NPAIR)
                        high(split_input(act, par, it), g - 5)
                for g in range(NPAIR - 2, NPAIR):
                    exponentials(g)

                def queries(g):
                    act.wait_ge(e_filled, n * NE + NPAIR + g + 1)
                    wait_count(act, x_filled, n * NPAIR + (g - 1 if g >= 2 else 0))
                    nc.scalar.copy(qnhi[:, g % 2], ebank(NPAIR + g)).then_inc(e_freed, 1)

                for g in range(2):
                    queries(g)
                act.wait_ge(m_filled, n + 1)
                act.wait_ge(rk_ready, n + 1)
                wait_count(act, mtlo_ready, n * CT)
                wait_count(act, x_filled, n * NPAIR)
                for h in range(CT):
                    nc.scalar.activation(mthi[:, h], kx[:, 1, h * C:(h + 1) * C], ACT.Copy, scale=rk[:, h:h + 1]
                                         ).then_inc(mthi_ready, 1)
                for g in range(2, NPAIR):
                    queries(g)

            for par in range(2):
                image(par, par, 0, True)
            with act.Fori(1, NIMG // 2 - 1) as it:
                for par in range(2):
                    image(2 * it + par, par, it, True)
            for par in range(2):
                image(NIMG - 2 + par, par, NIMG // 2 - 1, par == 0)

        @block.gpsimd
        def _(pool):
            def low(n, par, s):
                pool.wait_ge(hi_ready, n * PIECES + s + 1)
                nc.gpsimd.tensor_tensor(piece(xlo, par, s), piece(xs, par, s), piece(xhi, par, s).bitcast(F32),
                                        ALU.subtract).then_inc(lo_ready, 1)

            for s in range(PIECES):
                low(0, 0, s)

            def image(n, par, nxt):
                for g in range(NPAIR):
                    pool.wait_ge(q_recip, n * NPAIR + g + 1)
                    qh = qs[:, g].rearrange("p t h d -> p (t h) d")
                    nc.gpsimd.tensor_tensor(qh, qh, qrc[:, g % 2].rearrange("p (h o) -> p h o", o=1).to_broadcast(
                        [P, 2 * HEADS0, HD0]), ALU.mult).then_inc(q_ready, 1)
                if nxt:
                    for s in range(PIECES):
                        low(n + 1, 1 - par, s)

            for par in range(2):
                image(par, par, True)
            with pool.Fori(1, NIMG // 2 - 1) as it:
                for par in range(2):
                    image(2 * it + par, par, True)
            for par in range(2):
                image(NIMG - 2 + par, par, par == 0)

        @block.vector
        def _(dve):
            dve.wait_ge(w_hi, 1)
            nc.vector.tensor_tensor(wlo[:], wkqv[:], whi[:].bitcast(F32), ALU.subtract).then_inc(w_lo, 1)

            dve.wait_ge(w_in, 16 * NW)

            def image(n, par):
                def values(g):
                    dve.wait_ge(qv_filled, n * NPAIR + g + 1)
                    if g == 0:
                        wait_count(dve, ctx_step, n * NPAIR)
                    nc.vector.tensor_tensor(vT[:, 2 * g:2 * g + 2, :], qv[:, 2 * (g % 2):2 * (g % 2) + 2, C:2 * C],
                                            bqv[:, 1:2, :].to_broadcast([P, 2, C]), ALU.add).then_inc(v_done, 1)

                def shift_q(g):
                    if g == 0:
                        wait_count(dve, e_filled, n * NE)
                    q = qs[:, g].rearrange("p t h d -> p t (h d)")
                    qh = qs[:, g].rearrange("p t h d -> p (t h) d")
                    nc.vector.tensor_tensor(q, qv[:, 2 * (g % 2):2 * (g % 2) + 2, 0:C],
                                            bqv[:, 0:1, :].to_broadcast([P, 2, C]), ALU.add).then_inc(q_added, 1)
                    dve.wait_ge(q_added, n * NPAIR + g + 1)
                    nc.vector.tensor_reduce(qmx[:, g % 2], qh, AX.X, ALU.max).then_inc(q_maxed, 1)
                    dve.wait_ge(q_maxed, n * NPAIR + g + 1)
                    nc.vector.tensor_tensor(qh, qh, qmx[:, g % 2].rearrange("p (h o) -> p h o", o=1).to_broadcast(
                        [P, 2 * HEADS0, HD0]), ALU.subtract).then_inc(q_shifted, 1)

                def sum_q(g):
                    qh = qs[:, g].rearrange("p t h d -> p (t h) d")
                    dve.wait_ge(q_exp, n * NPAIR + g + 1)
                    nc.vector.tensor_reduce(qsm[:, g % 2], qh, AX.X, ALU.add).then_inc(q_summed, 1)
                    dve.wait_ge(q_summed, n * NPAIR + g + 1)
                    wait_count(dve, q_ready, n * NPAIR + g - 1)
                    nc.vector.reciprocal(qrc[:, g % 2], qsm[:, g % 2]).then_inc(q_recip, 1)

                def low_q(g):
                    dve.wait_ge(e_freed, n * NE + NPAIR + g + 1)
                    wait_count(dve, x_filled, n * NPAIR + (g - 1 if g >= 2 else 0))
                    nc.vector.tensor_tensor(qnlo[:, g % 2], ebank(NPAIR + g), qnhi[:, g % 2].bitcast(F32),
                                            ALU.subtract).then_inc(qnlo_ready, 1)

                def add_x(g):
                    dve.wait_ge(x_filled, n * NPAIR + g + 1)
                    for m in range(CT):
                        xt = xs[:, par, m, g * PAIR:(g + 1) * PAIR]
                        last = nc.vector.scalar_tensor_tensor(out=xt, in0=kx[:, g % 2, m * PAIR:(m + 1) * PAIR],
                                                              scalar=bkp[:, 1, m:m + 1], in1=xt,
                                                              op0=ALU.add, op1=ALU.add)
                    last.then_inc(x1_done, 1)

                wait_count(dve, exp_done, n * CT)
                for m in range(CT):
                    dve.wait_ge(k_freed, n * NK + (m + 1) * NCH)
                    nc.vector.tensor_reduce(nmax[:, m:m + 1], keys[:, m, :], AX.X, ALU.max,
                                            negate=True).then_inc(nmax_ready, 1)
                for g in range(NPAIR):
                    values(g)
                    shift_q(g)
                    if g >= 1:
                        sum_q(g - 1)
                sum_q(NPAIR - 1)
                dve.wait_ge(exp_done, (n + 1) * CT)
                wait_count(dve, mthi_ready, n * CT)
                wait_count(dve, mtlo_ready, n * CT)
                nc.vector.reciprocal(rk[:], ksum[:]).then_inc(rk_ready, 1)
                dve.wait_ge(ctx_step, (n + 1) * NPAIR)
                nc.vector.tensor_tensor(ctxm[:], kx[:, 0, 0:CT * P].rearrange("p (h k) -> p h k", h=CT),
                                        mask32[:].rearrange("p (o k) -> p o k", o=1).to_broadcast([P, CT, P]),
                                        ALU.mult).then_inc(ctx_masked, 1)
                low_q(0)
                low_q(1)
                dve.wait_ge(rk_ready, n + 1)
                dve.wait_ge(mthi_ready, (n + 1) * CT)
                for h in range(CT):
                    nc.vector.scalar_tensor_tensor(out=mtlo[:, h], in0=kx[:, 1, h * C:(h + 1) * C], scalar=rk[:, h:h + 1],
                                                   in1=mthi[:, h].bitcast(F32), op0=ALU.mult, op1=ALU.subtract
                                                   ).then_inc(mtlo_ready, 1)
                for g in range(NPAIR):
                    if 1 <= g < NPAIR - 1:
                        low_q(g + 1)
                    add_x(g)

            for par in range(2):
                image(par, par)
            with dve.Fori(1, NIMG // 2) as it:
                for par in range(2):
                    image(2 * it + par, par)


def phase_l1(nc, dram, sem, bnst, q, x1, work, early):
    with ExitStack() as ctx:
        def sb(name, shape, dtype=F32):
            return ctx.enter_context(nc.sbuf_tensor(name, shape, dtype))

        def ps(name, shape):
            return ctx.enter_context(nc.psum_tensor(name, shape, F32))

        wqkv = sb("wqkv", [P, CT, NU, P])
        wproj = sb("wproj", [P, 4, C])
        pwbd = sb("pwbd", [P, NU, P])
        dws = sb("dws", [P, NU, SCALE5 * SCALE5])
        pw4 = sb("pw4", [P, NU * 4, 32])
        dw4 = sb("dw4", [P, NU * 4, DY_PE])
        w4 = sb("w4", [P, NU * 4, DY_PE, 32])
        ident = sb("ident1", [P, P])
        mask8 = sb("mask8", [P, P])
        headsel = sb("headsel", [P, 2, 32])
        spread = sb("spread", [P, 2, 4, P], F32R)
        rep, kva, qpad, acc = cut(work, (2, 4, RROWS * WP), (2, HW), (2, HP * WP + NSH), (2, HW))
        kvT = sb("kvT", [P, 2, 2, 2, P + 1])
        vkraw = sb("vkraw", [P, 2, P + 1])
        vkm = sb("vkm", [P, 2, P])
        vkmT = sb("vkmT", [P, 2, P])
        dsel = sb("dsel", [P, 4, 2, 32])
        mt = sb("mt1", [P, 4, C])
        rhi = sb("rhi", [P, 2, CHUNK], F32R)
        rlo = sb("rlo", [P, 2, CHUNK], F32R)
        rcp = acc[:, 1]

        pj = ps("pj", [P, 2, 512])
        cv = ps("cv", [P, 2, 512])
        tr = ps("tr", [P, 2, 512])
        vk = ps("vk", [P, 512])
        ao = ps("ao", [P, 512])

        (w_in, w_first, x_in, zeroed, ones_set, w4_ready, pj_filled, pj_freed, rep_in0, rep_in1, tap_done,
         cv_filled, cv_freed, tr_filled, tr_freed, vk_step, vk_freed,
         vkm_ready, dsel_ready, sa_filled, sa_freed, sb_filled, sb_freed, den_filled, den_freed, r_ready,
         bc_filled, bc_freed, q_copied, rhi_ready, rlo_ready, spread_ready, y_filled, y_freed, bn_done, y_out) = (
            sem(f"l1_{n}") for n in (
                "w_in w_first x_in zeroed ones_set w4_ready pj_filled pj_freed rep_in0 rep_in1 tap_done "
                "cv_filled cv_freed tr_filled tr_freed vk_step vk_freed "
                "vkm_ready dsel_ready sa_filled sa_freed sb_filled sb_freed den_filled den_freed r_ready "
                "bc_filled bc_freed q_copied rhi_ready rlo_ready spread_ready y_filled y_freed bn_done y_out").split())
        rep_in = (rep_in0, rep_in1)
        NFIRST, NW = 4, 6
        NDEN = NCH // 2
        Y_CHUNKS = {0: (0, 1), 2: (2, 3), 3: (4, 5)}

        spread_raw = acc[:, 1, 0:8 * P].rearrange("p (c j h) -> p c j h", c=2, j=4)

        def padded(b):
            return qpad[:, b, 0:HP * WP].rearrange("p (r c) -> p r c", r=HP)

        def bc_bank(j):
            return (pj if j < 2 else cv)[:, j % 2]

        def y_bank(k):
            return (tr if k % 4 < 2 else cv)[:, k % 2]

        def shares(groups):
            return [range(groups * c // NCH, groups * (c + 1) // NCH) for c in range(NCH)]

        def unit_at(i, u):
            return (i, u) if u < NU else (i + 1, u - NU)

        block = ctx.enter_context(nc.Block())

        @block.sync
        def _(sp):
            for dst, name in ((wqkv, "wqkv"), (dws, "dws"), (pw4, "pw4"), (dw4, "dw4")):
                sp.dma_start(dst[:], dram[name]).then_inc(w_first, 16)
            sp.dma_start(x1[:], dram["x1"][0]).then_inc(x_in, 16)
            sp.dma_start(spread_raw, dram["spread"]).then_inc(w_in, 16)
            for dst, name in ((wproj, "wproj"), (pwbd, "pwbd"), (ident, "ident"), (mask8, "mask8"),
                              (headsel, "headsel")):
                sp.dma_start(dst[:], dram[name]).then_inc(w_in, 16)

            def image(i, nxt):
                for u in range(NU):
                    v_proj = settle(sp, i * (NU * NCH) + (u + 1) * NCH)
                    v_half = [settle(sp, (NU * i + u - 1) * NCH + 3 * (h + 1))
                              for h in range(2)]
                    if u - 2 in Y_CHUNKS and not (isinstance(i, int) and i == 0):
                        chunks = Y_CHUNKS[u - 2]
                        v_y = settle(sp, 2 * NCH * (i - 1) + 2 * (chunks[-1] + 1))
                        at = settle(sp, i - 1)
                        sp.wait_ge(y_freed, v_y)
                        store_y(at, chunks)
                    if u == NU - 1 and nxt:
                        v_x = settle(sp, i * (NU * NCH) + NU * NCH)
                        at = settle(sp, i + 1)
                        sp.wait_ge(pj_filled, v_x)
                        sp.dma_start(x1[:], image_of(dram["x1"], at)).then_inc(x_in, 16)
                    sp.wait_ge(pj_freed, v_proj)
                    for h in range(2):
                        wait_count(sp, cv_filled, v_half[h])
                        for b in range(4):
                            for s in range(NSH):
                                first = h * HALF * WP + s
                                sp.dma_start(rep[32 * s:32 * s + 32, h, b, :],
                                             qpad[32 * b:32 * b + 32, u % 2, first:first + RROWS * WP]
                                             ).then_inc(rep_in[h], 16)

            def store_y(at, chunks):
                span = slice(chunks[0] * CHUNK, (chunks[-1] + 1) * CHUNK)
                sp.dma_start(image_of(dram["y"], at)[:, :, span], q[:, 2:4, span]).then_inc(y_out, 16)

            image(0, True)
            with sp.Fori(1, NIMG - 1) as i:
                image(i, True)
            image(NIMG - 1, False)
            sp.wait_ge(y_out, 16 * len(Y_CHUNKS) * (NIMG - 1))
            sp.wait_ge(cv_filled, NIMG * NU * NCH)
            sp.wait_ge(tr_filled, NIMG * NTR)
            sp.wait_ge(q_copied, 2 * NIMG)
            for n, (y, x, loaded) in enumerate(early):
                sp.dma_start(y, dram["y"][n]).then_inc(loaded, 16)
                if x is not None:
                    sp.dma_start(x, dram["x1"][n]).then_inc(loaded, 16)

        @block.tensor
        def _(pe):
            pe.wait_ge(w_first, 16 * NFIRST)

            def project(i, u, chunks=range(NCH)):
                if u == 0:
                    pe.wait_ge(x_in, 16 * i + 16)
                for c in chunks:
                    g = i * (NU * NCH) + u * NCH + c
                    wait_count(pe, pj_freed, g - 1)
                    if u == 2 and c == 0:
                        wait_count(pe, bc_freed, 4 * NCH * i)
                    for kc in range(CT):
                        mm = nc.tensor.matmul(pj[:, c % 2, :CHUNK], wqkv[:, kc, u, :],
                                              x1[:, kc, c * CHUNK:(c + 1) * CHUNK],
                                              start=(kc == 0), stop=(kc == CT - 1))
                    mm.then_inc(pj_filled, 1)

            def convolve(i, u, chunks=range(NCH)):
                for c in chunks:
                    half, row = c // (NCH // 2), 8 * (c % (NCH // 2))
                    if c % (NCH // 2) == 0:
                        pe.wait_ge(rep_in[half], (i * NU + u + 1) * (16 * 16))
                    wait_count(pe, cv_freed, i * (NU * NCH) + u * NCH + c - 1)
                    if u == 0 and c == 0:
                        wait_count(pe, bc_freed, 4 * NCH * i)
                    if 1 <= u <= 3 and c == 0:
                        wait_count(pe, y_freed, 2 * NCH * i - (4 if u == 3 else 8))
                    if u == 4 and c == 0:
                        wait_count(pe, y_freed, 2 * NCH * i)
                    for b in range(4):
                        taps = rep[:, half, b, :].rearrange("p (r c) -> p r c", c=WP)
                        for dy in range(DY_PE):
                            nc.tensor.matmul(cv[32 * b:32 * b + 32, c % 2, :CHUNK], w4[:, 4 * u + b, dy, :],
                                             taps[:, row + dy:row + dy + 8, 0:W],
                                             start=(dy == 0), stop=False, skip_group_check=True)
                    if c == 0:
                        pe.wait_ge(tap_done, (i * NU + u + 1) * NT)
                    mm = nc.tensor.matmul(cv[:, c % 2, :CHUNK], pwbd[:, u, :], acc[:, u % 2, c * CHUNK:(c + 1) * CHUNK],
                                          start=False, stop=True, skip_group_check=True)
                    mm.then_inc(cv_filled, 1)

            def product(i, p, groups):
                u, source, half = PRODUCTS[p]
                last = (DG if source == 0 else AG) - 1
                base = i * NTR + SEG[p]

                def step(g):
                    pe.wait_ge(tr_freed, base + g + 1)
                    if g == 0:
                        wait_count(pe, vk_freed, i * 4 + p)
                        pe.wait_ge(ones_set, 1)
                    for t in range(2):
                        mm = nc.tensor.matmul(vk[:, 0:P + 1], kvT[:, g % 2, 0, t, 0:P], kvT[:, g % 2, 1, t, :],
                                              start=(g == 0 and t == 0), stop=(g == last and t == 1))
                    mm.then_inc(vk_step, 1)

                for g in groups:
                    if g == 0 and source == 0:
                        pe.wait_ge(pj_freed, i * (NU * NCH) + (u + 2) * NCH)
                    if g == 0 and source == 1:
                        pe.wait_ge(cv_freed, i * (NU * NCH) + (u + 2) * NCH)
                    wait_count(pe, tr_freed, base + (g - 1 if g >= 2 else 0))
                    if g == 0 and p:
                        wait_count(pe, y_freed, 2 * NCH * i - (8 if p < 3 else 0))
                    for t in range(2):
                        for kv in range(2):
                            if source == 0:
                                first = DFIRST + (2 * g + t) * P
                                src = qpad[:, kv, first:first + P]
                            else:
                                src = kva[:, kv, (2 * g + t) * P:(2 * g + t + 1) * P]
                            mm = nc.tensor.transpose(tr[:, g % 2, (2 * kv + t) * P:(2 * kv + t + 1) * P], src, ident[:])
                    mm.then_inc(tr_filled, 1)
                    if g >= 1:
                        step(g - 1)
                    if g == last:
                        step(g)

            def turn_product(i, p):
                pe.wait_ge(vkm_ready, 4 * i + p + 1)
                if p == 1:
                    pe.wait_ge(sa_freed, 4 * i + p)
                else:
                    wait_count(pe, sb_freed, 4 * i + p)
                nc.tensor.transpose(ao[:, 0:P], vkm[:, p % 2, :], ident[:]).then_inc(sa_filled, 1)

            def project_product(i, p):
                pe.wait_ge(sa_freed, 4 * i + max(p + 1, 2))
                wait_count(pe, sb_freed, 4 * i + p)
                nc.tensor.matmul(ao[:, P:P + C], vkmT[:, p % 2, :], wproj[:, slot_of(p), :],
                                 start=True, stop=True, skip_group_check=True).then_inc(sb_filled, 1)

            def denominators(i, d):
                if d == 0:
                    pe.wait_ge(sb_freed, 4 * i + 4)
                    pe.wait_ge(dsel_ready, 4 * i + 4)
                    pe.wait_ge(cv_freed, (i + 1) * NU * NCH)
                    pe.wait_ge(q_copied, 2 * (i + 1))
                else:
                    pe.wait_ge(den_freed, i * NDEN + d)
                for j in range(4):
                    for e in range(2):
                        c = 2 * d + e
                        mm = nc.tensor.matmul(ao[32 * j:32 * j + 32, 0:CHUNK], dsel[:, j, e, :],
                                              q[:, j, c * CHUNK:(c + 1) * CHUNK], start=(e == 0), stop=(e == 1),
                                              skip_group_check=True)
                mm.then_inc(den_filled, 1)

            def attend(i, between):
                def group(*gs):
                    if between:
                        product(i + 1, 0, gs)

                denominators(i, 0)
                group(0, 1)
                denominators(i, 1)
                group(2, 3)
                for c in range(NCH):
                    d = c // 2
                    if c % 2 == 0:
                        pe.wait_ge(rhi_ready, i * NDEN + d + 1)
                        pe.wait_ge(rlo_ready, i * NDEN + d + 1)
                    for j in range(4):
                        if c >= 1:
                            pe.wait_ge(bc_freed, 4 * NCH * i + 4 * c + j - 3)
                        elif j == 0 and between:
                            pe.wait_ge(pj_freed, (i + 1) * (NU * NCH) + 2 * NCH)
                        nc.tensor.matmul(bc_bank(j)[:, :CHUNK], spread[:, c % 2, j, :], rhi[:, d % 2, :],
                                         start=True, stop=False)
                        nc.tensor.matmul(bc_bank(j)[:, :CHUNK], spread[:, c % 2, j, :], rlo[:, d % 2, :],
                                         start=False, stop=True).then_inc(bc_filled, 1)
                    if c == 0:
                        denominators(i, 2)
                    group(c + 4)

            def output(i, chunks, u):
                pe.wait_ge(bc_freed, 4 * NCH * (i + 1))
                if u is not None:
                    pe.wait_ge(tr_freed, (i + 1) * NTR + (DG if u == 0 else SEG[3]))
                    pe.wait_ge(cv_freed, (i + 1) * (NU * NCH) + (u + 1) * NCH)
                for c in chunks:
                    for m in range(CT):
                        k = 2 * c + m
                        if c >= chunks[0] + 2:
                            pe.wait_ge(y_freed, 2 * NCH * i + k - 3)
                        for j in range(4):
                            mm = nc.tensor.matmul(y_bank(k)[:, :CHUNK], mt[:, j, m * P:(m + 1) * P],
                                                  q[:, j, c * CHUNK:(c + 1) * CHUNK], start=(j == 0), stop=(j == 3))
                        mm.then_inc(y_filled, 1)

            def image(i, prev, nxt):
                for u in range(NU):
                    if u == 0 and prev:
                        attend(i - 1, True)
                    elif u == 0:
                        product(i, 0, range(DG))
                    for c in range(NCH):
                        convolve(i, u, [c])
                        if u == 2:
                            product(i, 2, shares(DG)[c])
                        if u == 5:
                            product(i, 3, shares(AG)[c])
                    if u == 4:
                        turn_product(i, 2)
                    for c in range(NCH):
                        if u + 2 < NU or nxt:
                            project(*unit_at(i, u + 2), [c])
                        if u == 1:
                            product(i, 1, shares(AG)[c])
                    if u in Y_CHUNKS and prev:
                        output(i - 1, Y_CHUNKS[u], u)
                    if u == 1:
                        turn_product(i, 0)
                    if u == 2:
                        turn_product(i, 1)
                    if u == 3:
                        project_product(i, 0)
                        project_product(i, 1)
                    if u == 4:
                        project_product(i, 2)
                    if u == 5:
                        turn_product(i, 3)
                        project_product(i, 3)

            project(0, 0)
            project(0, 1)
            pe.wait_ge(w_in, 16 * NW)
            pe.wait_ge(w4_ready, 1)
            pe.wait_ge(spread_ready, 1)
            image(0, False, True)
            with pe.Fori(1, NIMG - 1) as i:
                image(i, True, True)
            image(NIMG - 1, True, False)
            attend(NIMG - 1, False)
            output(NIMG - 1, range(NCH), None)

        @block.scalar
        def _(act):
            act.wait_ge(zeroed, 1)

            def project(i, u, chunks=range(NCH)):
                if chunks[0] == 0 and not (isinstance(i, int) and i == 0 and u < 2):
                    act.wait_ge(tap_done, (i * NU + u - 1) * NT)
                    for h in range(2):
                        act.wait_ge(rep_in[h], (i * NU + u - 1) * 256)
                    if u in (0, 1):
                        act.wait_ge(tr_filled, i * NTR - AG)
                    if u in (2, 3):
                        act.wait_ge(tr_filled, i * NTR + DG)
                    if u in (4, 5):
                        act.wait_ge(tr_filled, i * NTR + SEG[3])
                    if u == 0 or u == 1:
                        wait_count(act, q_copied, 2 * (i - 1) + u + 1)
                for c in chunks:
                    act.wait_ge(pj_filled, i * (NU * NCH) + u * NCH + c + 1)
                    src = pj[:, c % 2, :CHUNK]
                    dst = padded(u % 2)[:, PAD + 8 * c:PAD + 8 * c + 8, PAD:PAD + W]
                    nc.scalar.copy(dst, src.rearrange("p (r c) -> p r c", c=W)).then_inc(pj_freed, 1)

            def copy_queries(i, u):
                act.wait_ge(pj_freed, i * (NU * NCH) + (u + 1) * NCH)
                wait_count(act, y_filled, 2 * NCH * i)
                nc.scalar.activation(q[:, HALVES[u]].rearrange("p (r c) -> p r c", c=W),
                                     padded(u % 2)[:, PAD:PAD + H, PAD:PAD + W], ACT.Relu).then_inc(q_copied, 1)

            def convolve(i, u, chunks=range(NCH)):
                if chunks[0] == 0:
                    if u < 4:
                        wait_count(act, tr_filled, i * NTR + (SEG[2] if u >= 2 else 0))
                    else:
                        wait_count(act, y_out, 16 * len(Y_CHUNKS) * i)
                for c in chunks:
                    if u == 4:
                        wait_count(act, bn_done, 2 * NCH * (i - 1) + 2 * c + 2)
                    act.wait_ge(cv_filled, i * (NU * NCH) + u * NCH + c + 1)
                    span = slice(c * CHUNK, (c + 1) * CHUNK)
                    if PARTS[u] == 0:
                        dst = q[:, 2 + HALVES[u], span]
                    else:
                        dst = kva[:, PARTS[u] - 1, span]
                    nc.scalar.activation(dst, cv[:, c % 2, :CHUNK], ACT.Copy if PARTS[u] == 2 else ACT.Relu
                                         ).then_inc(cv_freed, 1)

            def product(i, p, groups):
                _, source, _ = PRODUCTS[p]
                last = (DG if source == 0 else AG) - 1
                base = i * NTR + SEG[p]
                for g in groups:
                    act.wait_ge(tr_filled, base + g + 1)
                    wait_count(act, vk_step, base + (g - 1 if g >= 2 else 0))
                    bank = tr[:, g % 2, :].rearrange("p (x t c) -> p x t c", x=2, t=2)
                    if source == 0:
                        nc.scalar.activation(kvT[:, g % 2, 0, :, 0:P], bank[:, 0], ACT.Relu)
                        nc.scalar.copy(kvT[:, g % 2, 1, :, 0:P], bank[:, 1]).then_inc(tr_freed, 1)
                    else:
                        nc.scalar.copy(kvT[:, g % 2, :, :, 0:P], bank).then_inc(tr_freed, 1)
                    if g == last:
                        act.wait_ge(vk_step, base + last + 1)
                        wait_count(act, dsel_ready, 4 * i + p - 1)
                        nc.scalar.copy(vkraw[:, p % 2, :], vk[:, 0:P + 1]).then_inc(vk_freed, 1)

            def attend(i, between):
                groups = ((0, 1), (2, 3), (4, 5, 6))
                for d in range(NDEN):
                    if between:
                        product(i + 1, 0, groups[d])
                    act.wait_ge(r_ready, i * NDEN + d + 1)
                    wait_count(act, bc_filled, 4 * NCH * i + (8 if d == 2 else 0))
                    nc.scalar.copy(rhi[:, d % 2, :], rcp[:, d * CHUNK:(d + 1) * CHUNK]).then_inc(rhi_ready, 1)
                if between:
                    product(i + 1, 0, range(groups[-1][-1] + 1, DG))

            def turn_product(i, p):
                act.wait_ge(sa_filled, 4 * i + p + 1)
                nc.scalar.copy(vkmT[:, p % 2, :], ao[:, 0:P]).then_inc(sa_freed, 1)

            def project_product(i, p):
                act.wait_ge(sb_filled, 4 * i + p + 1)
                if not (isinstance(i, int) and i == 0):
                    act.wait_ge(y_filled, 2 * NCH * i)
                nc.scalar.copy(mt[:, slot_of(p), :], ao[:, P:P + C]).then_inc(sb_freed, 1)

            def output(i, chunks):
                for c in chunks:
                    for m in range(CT):
                        act.wait_ge(y_filled, 2 * NCH * i + 2 * c + 2)
                        nc.scalar.copy(q[:, 2 + m, c * CHUNK:(c + 1) * CHUNK], y_bank(2 * c + m)[:, :CHUNK]
                                       ).then_inc(y_freed, 1)

            def image(i, prev, nxt):
                for u in range(NU):
                    if u == 0 and prev:
                        attend(i - 1, True)
                    elif u == 0:
                        product(i, 0, range(DG))
                    for c in range(NCH):
                        convolve(i, u, [c])
                        if u == 2:
                            product(i, 2, shares(DG)[c])
                        if u == 5:
                            product(i, 3, shares(AG)[c])
                    if u == 4:
                        turn_product(i, 2)
                    for c in range(NCH):
                        if u + 2 < NU or nxt:
                            project(*unit_at(i, u + 2), [c])
                        if u == 1:
                            product(i, 1, shares(AG)[c])
                    if u in Y_CHUNKS and prev:
                        output(i - 1, Y_CHUNKS[u])
                    if u == 1:
                        turn_product(i, 0)
                    if u == 2:
                        turn_product(i, 1)
                    if u == 3:
                        project_product(i, 0)
                        project_product(i, 1)
                        copy_queries(i, 4)
                    if u == 4:
                        copy_queries(i, 5)
                        project_product(i, 2)
                    if u == 5:
                        turn_product(i, 3)
                        project_product(i, 3)

            project(0, 0)
            project(0, 1)
            act.wait_ge(w_in, 16 * NW)
            nc.scalar.copy(spread[:], spread_raw).then_inc(spread_ready, 1)
            image(0, False, True)
            with act.Fori(1, NIMG - 1) as i:
                image(i, True, True)
            image(NIMG - 1, True, False)
            attend(NIMG - 1, False)
            output(NIMG - 1, range(NCH))

        @block.gpsimd
        def _(pool):
            nc.gpsimd.memset(qpad[:], 0.0).then_inc(zeroed, 1)
            nc.gpsimd.memset(kvT[:, :, 1, :, P:P + 1], 1.0).then_inc(ones_set, 1)
            pool.wait_ge(w_in, 16 * NW)

            def image(i):
                for p in range(4):
                    pool.wait_ge(vk_freed, 4 * i + p + 1)
                    if p >= 2:
                        pool.wait_ge(sa_filled, 4 * i + p - 1)
                    else:
                        wait_count(pool, sa_filled, 4 * i)
                    nc.gpsimd.tensor_tensor(vkm[:, p % 2, :], vkraw[:, p % 2, 0:P], mask8[:], ALU.mult).then_inc(vkm_ready, 1)
                    wait_count(pool, den_filled, NDEN * i)
                    nc.gpsimd.tensor_tensor(dsel[:, slot_of(p)].rearrange("p e h -> p (e h)"),
                                            headsel[:].rearrange("p e h -> p (e h)"),
                                            vkraw[:, p % 2, P:P + 1].to_broadcast([P, 64]), ALU.mult
                                            ).then_inc(dsel_ready, 1)

            def attend(i):
                for d in range(NDEN):
                    pool.wait_ge(rhi_ready, i * NDEN + d + 1)
                    wait_count(pool, bc_filled, 4 * NCH * i + (8 if d == 2 else 0))
                    nc.gpsimd.tensor_tensor(rlo[:, d % 2, :], rcp[:, d * CHUNK:(d + 1) * CHUNK],
                                            rhi[:, d % 2, :].bitcast(F32), ALU.subtract).then_inc(rlo_ready, 1)

            image(0)
            with pool.Fori(1, NIMG) as i:
                attend(i - 1)
                image(i)
            attend(NIMG - 1)

        @block.vector
        def _(dve):
            dve.wait_ge(w_first, 16 * NFIRST)
            nc.vector.tensor_tensor(w4[:], pw4[:].rearrange("p b (o c) -> p b o c", o=1).to_broadcast([P, NU * 4, DY_PE, 32]),
                                    dw4[:].rearrange("p b (r o) -> p b r o", o=1).to_broadcast([P, NU * 4, DY_PE, 32]),
                                    ALU.mult).then_inc(w4_ready, 1)

            def taps(i, u, between=None):
                dve.wait_ge(pj_freed, i * (NU * NCH) + (u + 1) * NCH)
                wait_count(dve, cv_filled, (i * NU + u - 1) * NCH)
                a = acc[:, u % 2].rearrange("p (r c) -> p r c", c=W)
                for k, (dy, dx) in enumerate(DVE_TAPS):
                    if between and k == NT // 3:
                        between()
                    src = padded(u % 2)[:, dy:dy + H, dx:dx + W]
                    w = dws[:, u, SCALE5 * dy + dx:SCALE5 * dy + dx + 1]
                    if k == 0:
                        op = nc.vector.tensor_scalar(a, src, w, None, ALU.mult)
                    else:
                        dve.wait_ge(tap_done, (i * NU + u) * NT + k)
                        op = nc.vector.scalar_tensor_tensor(out=a, in0=src, scalar=w, in1=a, op0=ALU.mult, op1=ALU.add)
                    op.then_inc(tap_done, 1)

            def reciprocals(i, d):
                dve.wait_ge(den_filled, i * NDEN + d + 1)
                r = rcp[:, d * CHUNK:(d + 1) * CHUNK]
                nc.vector.tensor_scalar(r, ao[:, 0:CHUNK], EPS_ATT, None, ALU.add).then_inc(den_freed, 1)
                dve.wait_ge(den_freed, i * NDEN + d + 1)
                nc.vector.reciprocal(r, r).then_inc(r_ready, 1)

            def attend(i):
                reciprocals(i, 0)
                for c in range(NCH):
                    if c % 2 == 0 and c // 2 + 1 < NDEN:
                        reciprocals(i, c // 2 + 1)
                    for j in range(4):
                        k = 4 * c + j
                        dve.wait_ge(bc_filled, 4 * NCH * i + k + 1)
                        qc = q[:, j, c * CHUNK:(c + 1) * CHUNK]
                        nc.vector.tensor_tensor(qc, qc, bc_bank(j)[:, :CHUNK], ALU.mult).then_inc(bc_freed, 1)

            def statistics(i, chunks):
                for c in chunks:
                    for m in range(CT):
                        dve.wait_ge(y_freed, 2 * NCH * i + 2 * c + m + 1)
                        nc.vector.bn_stats(bnst_at(i, m, c), q[:, 2 + m, c * CHUNK:(c + 1) * CHUNK]).then_inc(bn_done, 1)

            def bnst_at(i, m, c):
                if isinstance(i, int):
                    return bnst[:, m, i, c, :]
                return bnst[:, m, bass.ds(i, 1), c, :].rearrange("p o s -> p (o s)")

            def image(i, prev):
                taps(i, 0)
                if prev:
                    attend(i - 1)
                if not prev:
                    dve.wait_ge(spread_ready, 1)
                for u in range(1, NU):
                    if prev and u - 2 in Y_CHUNKS:
                        taps(i, u, lambda: statistics(i - 1, Y_CHUNKS[u - 2]))
                    else:
                        taps(i, u)

            image(0, False)
            with dve.Fori(1, NIMG) as i:
                image(i, True)
            attend(NIMG - 1)
            statistics(NIMG - 1, range(NCH))


def phase_out(nc, dram, sem, bnst, q, x1, early):
    with ExitStack() as ctx:
        def sb(name, shape):
            return ctx.enter_context(nc.sbuf_tensor(name, shape, F32))

        xb = sb("xb", [P, 2, CT, HW])
        gb = sb("gb", [P, 2, CT])
        agg = sb("agg", [P, CT, 2])
        ve = sb("ve", [P, CT])
        rt = sb("rt", [P, CT])
        r0 = sb("r0", [P, CT])
        t0 = sb("t0", [P, CT])
        sc = sb("sc", [P, CT])
        sh = sb("sh", [P, CT])

        g_in, stat, root, load0, load4, scaled, summed, store0, store1, store2, store3, store4 = (
            sem(f"out_{n}") for n in
            "g_in stat root load0 load4 scaled summed store0 store1 store2 store3 store4".split())
        y_third, _, load3 = early[2]
        buffers = ((q[:, 2:4, :], x1[:], load0), *early[:2], (y_third, xb[:, 0], load3), (q[:, 0:2, :], xb[:, 1], load4))
        store = (store0, store1, store2, store3, store4)
        NB = len(buffers)
        order = (NIMG - 1, *range(NIMG - 1))

        block = ctx.enter_context(nc.Block())

        @block.sync
        def _(sp):
            sp.dma_start(gb[:], dram["gb"]).then_inc(g_in, 16)
            for k in range(len(early), NIMG):
                y, x, loaded = buffers[k % NB]
                if k >= NB:
                    sp.wait_ge(store[k % NB], 16 * (k // NB))
                if k > len(early):
                    sp.dma_start(y, dram["y"][order[k]]).then_inc(loaded, 16)
                sp.dma_start(x, dram["x1"][order[k]]).then_inc(loaded, 16)

        @block.gpsimd
        def _(pool):
            for k in range(NIMG):
                pool.wait_ge(summed, k + 1)
                pool.dma_start(dram["out"][order[k]], buffers[k % NB][0]).then_inc(store[k % NB], 16)
            for r in range(NB):
                pool.wait_ge(store[r], 16 * len(range(r, NIMG, NB)))

        @block.scalar
        def _(act):
            act.wait_ge(stat, CT + 1)
            nc.scalar.activation(rt[:], ve[:], ACT.Sqrt).then_inc(root, 1)
            act.wait_ge(stat, CT + 9)
            for k in range(NIMG):
                y, _, loaded = buffers[k % NB]
                if k:
                    act.wait_ge(loaded, 32 * (k // NB + (1 if k % NB else 0)))
                for m in range(CT):
                    last = nc.scalar.activation(y[:, m], y[:, m], ACT.Identity, bias=sh[:, m:m + 1], scale=sc[:, m:m + 1])
                last.then_inc(scaled, 1)

        @block.vector
        def _(dve):
            done = [0]

            def step(op):
                done[0] += 1
                op.then_inc(stat, 1)
                dve.wait_ge(stat, done[0])

            for m in range(CT):
                step(nc.vector.bn_aggr(agg[:, m], bnst[:, m].rearrange("p i c s -> p (i c s)")))
            step(nc.vector.tensor_scalar(ve[:], agg[:, :, 1], EPS_BN, None, ALU.add))
            dve.wait_ge(root, 1)
            dve.wait_ge(g_in, 16)
            step(nc.vector.reciprocal(r0[:], rt[:]))
            step(nc.vector.tensor_tensor(t0[:], r0[:], r0[:], ALU.mult))
            step(nc.vector.tensor_tensor(t0[:], t0[:], ve[:], ALU.mult))
            step(nc.vector.tensor_scalar(t0[:], t0[:], -0.5, 1.5, ALU.mult, ALU.add))
            step(nc.vector.tensor_tensor(r0[:], r0[:], t0[:], ALU.mult))
            step(nc.vector.tensor_tensor(sc[:], r0[:], gb[:, 0], ALU.mult))
            step(nc.vector.tensor_tensor(t0[:], agg[:, :, 0], sc[:], ALU.mult))
            nc.vector.tensor_tensor(sh[:], gb[:, 1], t0[:], ALU.subtract).then_inc(stat, 1)
            for k in range(NIMG):
                y, x, _ = buffers[k % NB]
                dve.wait_ge(scaled, k + 1)
                nc.vector.tensor_tensor(y, y, x, ALU.add).then_inc(summed, 1)


def build(nc, dram):
    with ExitStack() as ctx:
        def sem(name):
            return ctx.enter_context(nc.semaphore(name))

        bnst = ctx.enter_context(nc.sbuf_tensor("bnst", [P, CT, NIMG, NCH, 6], F32))
        phase_l0(nc, dram, sem)
        q = ctx.enter_context(nc.sbuf_tensor("q", [P, 4, HW], F32))
        x1 = ctx.enter_context(nc.sbuf_tensor("x1", [P, CT, HW], F32))
        work = ctx.enter_context(nc.sbuf_tensor("work", [P, 2 * 4 * RROWS * WP + 4 * HW + 2 * (HP * WP + NSH)], F32))
        parts = cut(work, *[(CT, HW)] * 5)
        early = ((parts[0], parts[1], sem("out_load1")), (parts[2], parts[3], sem("out_load2")),
                 (parts[4], None, sem("out_load3")))
        phase_l1(nc, dram, sem, bnst, q, x1, work, early)
        phase_out(nc, dram, sem, bnst, q, x1, early)


def layouts(inputs):
    import numpy as np

    a = {n: np.ascontiguousarray(v) for n, v in inputs.items()}

    def columns(v, parts):
        return v.reshape(parts, P).T

    out = {}
    out["x"] = a["x"].reshape(NIMG, CT, P, HW).transpose(0, 2, 1, 3)
    wkqv = np.concatenate([a["L0_conv_Wk"].T, a["L0_conv_Wq"].T, a["L0_conv_Wv"].T], 1)
    out["wkqv"] = wkqv.reshape(CT, P, 3 * C).transpose(1, 0, 2)
    out["wp"] = a["L0_conv_Wp"].T.reshape(CT, P, C).transpose(1, 0, 2)
    out["bqv"] = np.broadcast_to(np.stack([a["L0_conv_bq"], a["L0_conv_bv"]]), (P, 2, C))
    out["bkp"] = np.stack([columns(a["L0_conv_bk"], CT), columns(a["L0_conv_bp"], CT)], 1)

    rows = np.array([[3 * DIM * h + DIM * PARTS[u] + d for h in range(16 * HALVES[u], 16 * HALVES[u] + 16)
                      for d in range(DIM)] for u in range(NU)])
    wq = a["L1_conv_w_qkv"][rows]
    out["wqkv"] = wq.transpose(2, 0, 1).reshape(CT, P, NU, P).transpose(1, 0, 2, 3)
    out["wproj"] = a["L1_conv_w_proj"].T.reshape(4, P, C).transpose(1, 0, 2)
    pw = a["L1_conv_w_pw"][rows[:, ::DIM] // DIM]
    bd = np.zeros((NU, P, P), pw.dtype)
    for g in range(16):
        bd[:, 8 * g:8 * g + 8, 8 * g:8 * g + 8] = pw[:, g].transpose(0, 2, 1)
    out["pwbd"] = bd.transpose(1, 0, 2)
    blocks = np.stack([bd[:, 32 * b:32 * b + 32, 32 * b:32 * b + 32] for b in range(4)], 1)
    out["pw4"] = np.tile(blocks.reshape(NU * 4, 32, 32).transpose(1, 0, 2), (NSH, 1, 1))
    dw = a["L1_conv_w_dw"].reshape(-1, SCALE5, SCALE5)[rows]
    out["dws"] = dw.reshape(NU, P, SCALE5 * SCALE5).transpose(1, 0, 2)
    stack = dw[:, :, :DY_PE, :NSH].reshape(NU, 4, 32, DY_PE, NSH)
    out["dw4"] = stack.transpose(4, 2, 0, 1, 3).reshape(P, NU * 4, DY_PE)
    out["gb"] = np.stack([columns(a["L1_conv_bn_gamma"], CT), columns(a["L1_conv_bn_beta"], CT)], 1)

    k = np.arange(P)
    out["ident"] = np.eye(P, dtype=np.float32)
    out["mask32"] = (k[:, None] // HD0 == k[None] // HD0).astype(np.float32)
    out["mask8"] = (k[:, None] // DIM == k[None] // DIM).astype(np.float32)
    head = 16 * np.arange(2)[None, :, None] + k[:, None, None] // DIM
    out["headsel"] = (head == np.arange(32)[None, None]).astype(np.float32)
    j = np.arange(4)
    row, half = k[:, None, None, None], 16 * np.arange(2)[None, :, None, None]
    out["spread"] = ((row // 32 == j[None, None, :, None]) & (row % 32 == half + k[None, None, None] // DIM)
                     ).astype(np.float32)
    return {n: np.ascontiguousarray(v) for n, v in out.items()}


def kernel(**inputs):
    import numpy as _np
    import concourse.bacc as _bacc
    from concourse.bass_utils import run_bass_kernel_spmd as _run

    nc = _bacc.Bacc("TRN2", target_bir_lowering=False, num_devices=1)
    arrays, dram = {}, {}
    for name, a in layouts(inputs).items():
        arrays[f"in_{name}"] = a
        dram[name] = nc.dram_tensor(f"in_{name}", a.shape, mybir.dt.from_np(a.dtype), kind="ExternalInput").ap()
    for name in ("x1", "y"):
        dram[name] = nc.dram_tensor(f"scratch_{name}", (NIMG, P, CT, HW), F32).ap()
    dram["out"] = nc.dram_tensor("out_0", (NIMG, P, CT, HW), F32, kind="ExternalOutput").ap()
    build(nc, dram)
    r = _run(nc, [arrays], core_ids=[0])
    got = r.results[0]["out_0"]
    return _np.ascontiguousarray(got.transpose(0, 2, 1, 3)).reshape(NIMG, C, H, W)
```
